# Optimizing a Trainium2 kernel written in Bass

```python
import numpy as np
import jax
import jax.numpy as jnp

def _softmax(x, axis=-1):
    return jax.nn.softmax(x, axis=axis)

def _gelu(x):
    return jax.nn.gelu(x, approximate=True)

def _silu(x):
    return jax.nn.silu(x)

def _sigmoid(x):
    return jax.nn.sigmoid(x)

def _layernorm(x, axis=-1, eps=1e-05):
    m = jnp.mean(x, axis=axis, keepdims=True)
    v = jnp.var(x, axis=axis, keepdims=True)
    return (x - m) / jnp.sqrt(v + eps)

def _scatter_add(tgt, idx, src, axis=0):
    return tgt.at[idx].add(src)

def _segment_sum(src, seg, n):
    return jax.ops.segment_sum(src, seg, n)
kernel_name = 'mk_seq_preln_d1_jaxref_r4_3f6865'

def setup_inputs(seed: int=0):
    np.random.seed(seed)
    _w = jnp.asarray

    def _L0_attn_setup():
        import jax, jax.numpy as jnp
        import numpy as np
        NUM_HEADS = 16
        LN_EPS = 1e-05

        def _gelu(x):
            return jax.nn.gelu(x, approximate=False)
        key = jax.random.key(seed)
        ks = jax.random.split(key, 12)
        B, S, E = (2, 512, 256)
        H = E // 2
        s = lambda fan_in: 1.0 / np.sqrt(fan_in)
        inp = {'x': jax.random.normal(ks[0], (B, S, E), jnp.float32), 'Wq': jax.random.normal(ks[1], (E, E), jnp.float32) * s(E), 'bq': jnp.zeros((E,), jnp.float32), 'Wk': jax.random.normal(ks[2], (E, E), jnp.float32) * s(E), 'bk': jnp.zeros((E,), jnp.float32), 'Wv': jax.random.normal(ks[3], (E, E), jnp.float32) * s(E), 'bv': jnp.zeros((E,), jnp.float32), 'Wo': jax.random.normal(ks[4], (E, E), jnp.float32) * s(E), 'bo': jnp.zeros((E,), jnp.float32), 'dp_w1': jax.random.normal(ks[5], (E, H), jnp.float32) * s(E), 'dp_b1': jnp.zeros((H,), jnp.float32), 'ln_g': jnp.ones((H,), jnp.float32), 'ln_b': jnp.zeros((H,), jnp.float32), 'dp_w2': jax.random.normal(ks[6], (H, 1), jnp.float32) * s(H), 'dp_b2': jnp.zeros((1,), jnp.float32), 'g_w1': jax.random.normal(ks[7], (1, 16), jnp.float32), 'g_b1': jnp.zeros((16,), jnp.float32), 'g_w2': jax.random.normal(ks[8], (16, 1), jnp.float32) * s(16), 'g_b2': jnp.zeros((1,), jnp.float32)}
        return inp
    _L0_attn_in = _L0_attn_setup()

    def _L0_ffn_setup():
        import jax, jax.numpy as jnp
        import numpy as np
        TOP_K = 2
        N_GROUP = 4
        TOPK_GROUP = 2
        SCALE = 2.5
        B, S, D = (2, 512, 256)
        E, F = (8, 128)
        SH = 256

        def _moe_gate(x2d, gate_w, gate_bias):
            T = x2d.shape[0]
            logits = x2d.astype(jnp.float32) @ gate_w.T.astype(jnp.float32)
            scores = jax.nn.sigmoid(logits)
            sc = scores + gate_bias[None, :]
            grp = sc.reshape(T, N_GROUP, E // N_GROUP)
            group_scores = jax.lax.top_k(grp, 2)[0].sum(-1)
            gidx = jax.lax.top_k(group_scores, TOPK_GROUP)[1]
            gmask = jnp.zeros((T, N_GROUP), sc.dtype).at[jnp.arange(T)[:, None], gidx].set(1.0)
            smask = jnp.repeat(gmask, E // N_GROUP, axis=1)
            tmp = jnp.where(smask > 0, sc, 0.0)
            tidx = jax.lax.top_k(tmp, TOP_K)[1]
            tw = jnp.take_along_axis(scores, tidx, axis=1)
            tw = tw / (tw.sum(-1, keepdims=True) + 1e-20)
            return (tidx, tw * SCALE)
        key = jax.random.key(seed)
        ks = jax.random.split(key, 10)
        w = 0.02
        return {'hidden_states': jax.random.normal(ks[0], (B, S, D), jnp.float32), 'gate_w': jax.random.normal(ks[1], (E, D), jnp.float32) * w, 'gate_bias': jax.random.normal(ks[2], (E,), jnp.float32) * 0.01, 'w1': jax.random.normal(ks[3], (E, F, D), jnp.float32) * w, 'w2': jax.random.normal(ks[4], (E, D, F), jnp.float32) * w, 'w3': jax.random.normal(ks[5], (E, F, D), jnp.float32) * w, 'shared_gate_w': jax.random.normal(ks[6], (SH, D), jnp.float32) * w, 'shared_up_w': jax.random.normal(ks[7], (SH, D), jnp.float32) * w, 'shared_down_w': jax.random.normal(ks[8], (D, SH), jnp.float32) * w}
    _L0_ffn_in = _L0_ffn_setup()
    _d = {'L0_attn_x': _L0_attn_in['x'], 'L0_attn_Wq': _L0_attn_in['Wq'], 'L0_attn_bq': _L0_attn_in['bq'], 'L0_attn_Wk': _L0_attn_in['Wk'], 'L0_attn_bk': _L0_attn_in['bk'], 'L0_attn_Wv': _L0_attn_in['Wv'], 'L0_attn_bv': _L0_attn_in['bv'], 'L0_attn_Wo': _L0_attn_in['Wo'], 'L0_attn_bo': _L0_attn_in['bo'], 'L0_attn_dp_w1': _L0_attn_in['dp_w1'], 'L0_attn_dp_b1': _L0_attn_in['dp_b1'], 'L0_attn_ln_g': _L0_attn_in['ln_g'], 'L0_attn_ln_b': _L0_attn_in['ln_b'], 'L0_attn_dp_w2': _L0_attn_in['dp_w2'], 'L0_attn_dp_b2': _L0_attn_in['dp_b2'], 'L0_attn_g_w1': _L0_attn_in['g_w1'], 'L0_attn_g_b1': _L0_attn_in['g_b1'], 'L0_attn_g_w2': _L0_attn_in['g_w2'], 'L0_attn_g_b2': _L0_attn_in['g_b2'], 'L0_ffn_gate_w': _L0_ffn_in['gate_w'], 'L0_ffn_gate_bias': _L0_ffn_in['gate_bias'], 'L0_ffn_w1': _L0_ffn_in['w1'], 'L0_ffn_w2': _L0_ffn_in['w2'], 'L0_ffn_w3': _L0_ffn_in['w3'], 'L0_ffn_shared_gate_w': _L0_ffn_in['shared_gate_w'], 'L0_ffn_shared_up_w': _L0_ffn_in['shared_up_w'], 'L0_ffn_shared_down_w': _L0_ffn_in['shared_down_w']}
    _x0 = _d['L0_attn_x']
    _d['L0_attn_x'] = jax.random.normal(jax.random.fold_in(jax.random.key(seed), 1), (8, 1024, 256), dtype=_x0.dtype)
    del _x0
    return _d

def reference(L0_attn_x, L0_attn_Wq, L0_attn_bq, L0_attn_Wk, L0_attn_bk, L0_attn_Wv, L0_attn_bv, L0_attn_Wo, L0_attn_bo, L0_attn_dp_w1, L0_attn_dp_b1, L0_attn_ln_g, L0_attn_ln_b, L0_attn_dp_w2, L0_attn_dp_b2, L0_attn_g_w1, L0_attn_g_b1, L0_attn_g_w2, L0_attn_g_b2, L0_ffn_gate_w, L0_ffn_gate_bias, L0_ffn_w1, L0_ffn_w2, L0_ffn_w3, L0_ffn_shared_gate_w, L0_ffn_shared_up_w, L0_ffn_shared_down_w):

    def _L0_attn_ref(x, Wq, bq, Wk, bk, Wv, bv, Wo, bo, dp_w1, dp_b1, ln_g, ln_b, dp_w2, dp_b2, g_w1, g_b1, g_w2, g_b2):
        import jax, jax.numpy as jnp
        import numpy as np
        NUM_HEADS = 16
        LN_EPS = 1e-05

        def _gelu(x):
            return jax.nn.gelu(x, approximate=False)
        B, S, E = x.shape
        Hn = NUM_HEADS
        Dh = E // Hn
        scale = Dh ** (-0.5)
        Q = (x @ Wq + bq).reshape(B, S, Hn, Dh)
        K = (x @ Wk + bk).reshape(B, S, Hn, Dh)
        V = (x @ Wv + bv).reshape(B, S, Hn, Dh)
        logits = jnp.einsum('bqhd,bkhd->bhqk', Q, K) * scale
        causal = jnp.tril(jnp.ones((S, S), bool))
        logits = jnp.where(causal, logits, -jnp.inf)
        attn = jax.nn.softmax(logits, axis=-1)
        h = x @ dp_w1 + dp_b1
        mu = h.mean(-1, keepdims=True)
        var = ((h - mu) ** 2).mean(-1, keepdims=True)
        h = (h - mu) / jnp.sqrt(var + LN_EPS) * ln_g + ln_b
        drift = (_gelu(h) @ dp_w2 + dp_b2)[..., 0]
        g = _gelu(drift[..., None] * g_w1[0] + g_b1)
        gate = jnp.tanh(g @ g_w2 + g_b2)[..., 0]
        gated = attn * gate[:, None, None, :]
        out = jnp.einsum('bhqk,bkhd->bqhd', gated, V).reshape(B, S, E)
        return out @ Wo + bo

    def _L0_ffn_ref(hidden_states, gate_w, gate_bias, w1, w2, w3, shared_gate_w, shared_up_w, shared_down_w):
        import jax, jax.numpy as jnp
        import numpy as np
        TOP_K = 2
        N_GROUP = 4
        TOPK_GROUP = 2
        SCALE = 2.5
        B, S, D = (2, 512, 256)
        E, F = (8, 128)
        SH = 256

        def _moe_gate(x2d, gate_w, gate_bias):
            T = x2d.shape[0]
            logits = x2d.astype(jnp.float32) @ gate_w.T.astype(jnp.float32)
            scores = jax.nn.sigmoid(logits)
            sc = scores + gate_bias[None, :]
            grp = sc.reshape(T, N_GROUP, E // N_GROUP)
            group_scores = jax.lax.top_k(grp, 2)[0].sum(-1)
            gidx = jax.lax.top_k(group_scores, TOPK_GROUP)[1]
            gmask = jnp.zeros((T, N_GROUP), sc.dtype).at[jnp.arange(T)[:, None], gidx].set(1.0)
            smask = jnp.repeat(gmask, E // N_GROUP, axis=1)
            tmp = jnp.where(smask > 0, sc, 0.0)
            tidx = jax.lax.top_k(tmp, TOP_K)[1]
            tw = jnp.take_along_axis(scores, tidx, axis=1)
            tw = tw / (tw.sum(-1, keepdims=True) + 1e-20)
            return (tidx, tw * SCALE)
        b, s, d = hidden_states.shape
        x = hidden_states.reshape(-1, d)
        T = x.shape[0]
        tidx, tw = _moe_gate(x, gate_w, gate_bias)
        ew = jnp.zeros((T, E), x.dtype).at[jnp.arange(T)[:, None], tidx].add(tw.astype(x.dtype))
        h = jax.nn.silu(jnp.einsum('td,efd->tef', x, w1)) * jnp.einsum('td,efd->tef', x, w3)
        y = jnp.einsum('tef,edf,te->td', h, w2, ew)
        shared = jax.nn.silu(x @ shared_gate_w.T) * (x @ shared_up_w.T) @ shared_down_w.T
        return (y + shared).reshape(b, s, d)
    x = L0_attn_x
    x = x + _L0_attn_ref(_layernorm(x, axis=-1), L0_attn_Wq, L0_attn_bq, L0_attn_Wk, L0_attn_bk, L0_attn_Wv, L0_attn_bv, L0_attn_Wo, L0_attn_bo, L0_attn_dp_w1, L0_attn_dp_b1, L0_attn_ln_g, L0_attn_ln_b, L0_attn_dp_w2, L0_attn_dp_b2, L0_attn_g_w1, L0_attn_g_b1, L0_attn_g_w2, L0_attn_g_b2)
    x = x + _L0_ffn_ref(_layernorm(x, axis=-1), L0_ffn_gate_w, L0_ffn_gate_bias, L0_ffn_w1, L0_ffn_w2, L0_ffn_w3, L0_ffn_shared_gate_w, L0_ffn_shared_up_w, L0_ffn_shared_down_w)
    return x

_drawn_inputs = setup_inputs


def setup_inputs(seed=0):
    import zlib

    import numpy as np

    out = dict(_drawn_inputs(seed))
    spreads = {'L0_attn_bq': (0.0, 0.8),
     'L0_attn_bk': (0.0, 0.8),
     'L0_attn_bv': (0.0, 0.652),
     'L0_attn_bo': (0.0, 0.1),
     'L0_attn_dp_b1': (0.0, 0.8),
     'L0_attn_ln_g': (1.0, 0.6),
     'L0_attn_ln_b': (0.0, 0.8),
     'L0_attn_g_b1': (0.0, 0.774)}
    factors = {'L0_attn_Wq': 2.959,
     'L0_attn_Wk': 2.881,
     'L0_attn_dp_w1': 2.692,
     'L0_attn_g_w1': 3.357,
     'L0_ffn_gate_w': 3.11,
     'L0_ffn_gate_bias': 8.0,
     'L0_ffn_w1': 2.727,
     'L0_ffn_w2': 2.709,
     'L0_ffn_w3': 2.7,
     'L0_ffn_shared_gate_w': 3.431,
     'L0_ffn_shared_up_w': 3.397,
     'L0_ffn_shared_down_w': 3.397}
    for name, (base, spread) in spreads.items():
        noise = np.random.default_rng([zlib.crc32(name.encode()), seed]).standard_normal(out[name].shape)
        drawn = base * np.exp(spread * noise) if base else spread * noise
        out[name] = jnp.asarray(drawn.astype(out[name].dtype))
    for name, factor in factors.items():
        out[name] = (out[name] * factor).astype(out[name].dtype)
    return out
```

```python
from contextlib import ExitStack

import numpy as np

import concourse.bass as bass
from concourse import mybir

F32 = mybir.dt.float32
F32R = mybir.dt.float32r
ALU = mybir.AluOpType
ACT = mybir.ActivationFunctionType
X_AXIS = mybir.AxisListType.X

P = 128
B, S, E = 8, 1024, 256
H, DH = 16, 16
KE = E // P
TILES = S // P
GROUP = 4
GROUPS = H // GROUP
PAIRS = GROUP // 2
CHUNK = 512
CHUNKS = S // CHUNK
DP = 128
GH = 16
EXPERTS, F, SHARED = 8, 128, 2
BLOCKS = EXPERTS + SHARED
Q = 256
QS = S // Q
QT = Q // P
EPS = 1e-5
NEG = -1e30
ROUTE_SCALE = 2.5

STEPS = [(c, kt) for c in range(CHUNKS) for kt in range(TILES) if kt * P < (c + 1) * CHUNK]
NSTEP = len(STEPS)
MAXU = [(p, qt, kc, j) for p in range(PAIRS) for qt in range(TILES)
        for kc in range(qt // (CHUNK // P) + 1) for j in range(2)]
MAX_PER_BANK = len(MAXU) // 2

A_USES = 2 * TILES + 2 * KE * CHUNKS
CD_USES_Q = 2 * QT + 2 + BLOCKS + 1
CD_USES = QS * CD_USES_Q
ROUTE_OPS = 19


def step_queries(c, kt):
    q0 = max(c * CHUNK, kt * P)
    return q0, (c + 1) * CHUNK - q0


def max_keys(qt, kc):
    n = min(CHUNK, (qt + 1) * P - kc * CHUNK)
    return n, kc == qt // (CHUNK // P)


def cost(item):
    return {"AS": 3000, "AT": 600, "AV": 3072, "AQ": 4096, "CL": 1000, "CR": 1500, "CO": 1500,
            "CW": 2048, "CS": 1500, "CT": 600, "CG": 1200, "CE": 600, "H": 3072, "Y": 1536,
            "F": 1024}.get(item[0], 0)


def merge(a, b):
    ta, tb = sum(map(cost, a)) or 1, sum(map(cost, b)) or 1
    out, ia, ib, ca, cb = [], 0, 0, 0, 0
    while ia < len(a) or ib < len(b):
        if ib >= len(b) or (ia < len(a) and ca / ta <= cb / tb):
            ca += cost(a[ia])
            out.append(a[ia])
            ia += 1
        else:
            cb += cost(b[ib])
            out.append(b[ib])
            ib += 1
    return out


def projection_items(c):
    tiles = range(c * TILES // CHUNKS, (c + 1) * TILES // CHUNKS)
    out = [("AS", c)] + [("AT", t) for t in tiles]
    out += [("AX", c + 1)] if c + 1 < CHUNKS else []
    out += [("AV", t) for t in tiles] + [("AQ", c, u) for u in range(2 * KE)]
    return out


GATE = [(k,) for k in ("GA", "GB", "GC", "GD", "GE", "GF", "GG", "GH", "GI", "GJ", "GK", "GL")]


def output_items(q):
    return ([("CO", q)] + [("CW", q, i) for i in range(QT)] + [("CS", q)] + [("CT", q, i) for i in range(QT)]
            + [("CG", q), ("CR2", q), ("CE", q)])


def expert_items(q):
    order = list(range(EXPERTS, BLOCKS)) + list(range(EXPERTS))
    out = []
    for i in range(BLOCKS + 2):
        if i < BLOCKS:
            out.append(("H", q, i, order[i]))
        if i >= 2:
            out.append(("Y", q, i - 2, order[i - 2]))
    return out + [("YE", q), ("F", q)]


def side_items(project, finish):
    a0, a1 = (([("AX", 0)] + projection_items(0)), projection_items(1)) if project else ([], [])
    gate = GATE if project else []
    if not finish:
        return a0 + a1 + gate
    head = a0[:len(a0) // 2]
    rest = a0[len(a0) // 2:]
    out = head + [("CL",)] + rest[:3] + [("CR",)] + rest[3:]
    out += merge(output_items(0), a1)
    for q in range(QS):
        out += merge(expert_items(q), output_items(q + 1) if q + 1 < QS else [])
    spots = [i for i, it in enumerate(out) if it[0] == "H"][2:2 + len(gate)]
    for i, g in reversed(list(zip(spots, gate))):
        out.insert(i, g)
    return out


def max_items(units):
    return [("M", u) for u in units]


def batch_items(project, finish):
    side = [(it[0], -1 if it[0][0] in "CHYF" else 1) + it[1:] for it in side_items(project, finish)]
    attention = sum(6 * 2 * step_queries(*s)[1] for s in STEPS) * GROUPS
    total = attention + sum(cost(it) for it in side)
    items, done, at = [], 0, 0
    n_slots = GROUPS * NSTEP
    waiting = None

    def side_until(goal):
        nonlocal done, at
        while at < len(side) and done < goal and (side[at][0] != "CL" or ("OE", -1, GROUPS - 1, CHUNKS - 1) in items):
            done += cost(side[at])
            items.append(side[at])
            at += 1

    for g in range(GROUPS):
        nxt = (0, g + 1) if g + 1 < GROUPS else (1, 0)
        has_next = g + 1 < GROUPS or project
        if has_next:
            items.append(("LD",) + nxt)
        first, last = 1, NSTEP - 3
        per = -(-len(MAXU) // (last - first + 1))
        for s in range(NSTEP):
            slot = g * NSTEP + s
            units = []
            if has_next and first <= s <= last:
                lo = (s - first) * per
                units = [("M",) + nxt + (u,) for u in range(lo, min(lo + per, len(MAXU)))]
            half = len(units) // 2
            cols = 6 * 2 * step_queries(*STEPS[s])[1]
            goal = total * (slot + 1) / n_slots if finish else attention * (slot + 1) / n_slots + (
                total - attention) * min(1, (slot + 1) / (n_slots - 2 * NSTEP))
            items.append(("QK", 0, g, s, 0))
            items += units[:half]
            start = done
            done += cols
            side_until(start + cols + (goal - start - cols) / 2)
            items.append(("QK", 0, g, s, 1))
            items.append(("MSK", 0, g, s))
            if waiting:
                items.append(waiting)
                if waiting[3] == NSTEP - 1 or STEPS[waiting[3] + 1][1] == 0:
                    items.append(("OE",) + waiting[1:3] + (STEPS[waiting[3]][0],))
            elif finish:
                items += [("PV", -1, GROUPS - 1, NSTEP - 1), ("OE", -1, GROUPS - 1, CHUNKS - 1)]
            if slot == 0:
                items.append(("VA", 0, GROUPS - 1))
            waiting = ("PV", 0, g, s)
            items += units[half:]
            side_until(goal)
            if s == last and has_next:
                items.append(("MT",) + nxt)
            if project and slot in (n_slots - NSTEP + 1, n_slots - NSTEP + 2, n_slots - NSTEP + 3):
                items.append(("VA", 1, slot - (n_slots - NSTEP + 1)))
    side_until(10 ** 12)
    assert not finish or items.index(("CL", -1)) > items.index(("OE", -1, GROUPS - 1, CHUNKS - 1))
    return items


def build(nc, ins, out):
    x_in = ins["x"]
    with ExitStack() as ctx:
        def sb(name, shape, dt=F32):
            return ctx.enter_context(nc.sbuf_tensor(name, shape, dt))

        def psum(name, shape):
            return ctx.enter_context(nc.psum_tensor(name, shape, F32))

        def sem(name):
            return ctx.enter_context(nc.semaphore(name))

        def dram(name, shape, dt=F32):
            return nc.dram_tensor(name, shape, dt).ap()

        KINDS = ("q_hi", "q_lo", "k_hi", "k_lo")
        qk_s = dram("qk_s", (B * 4 * E, S))
        nm_s = dram("nm_s", (B * GROUPS * GROUP * TILES, P))
        o_s = dram("o_s", (B * GROUPS * P, S))
        li_s = dram("li_s", (B * H, S))
        ew_s = dram("ew_s", (B * EXPERTS, S))

        wq = sb("wq", [P, KE, E])
        wk = sb("wk", [P, KE, E])
        wvd = sb("wvd", [P, KE, E + DP])
        wo = sb("wo", [P, KE, E])
        w13_hi = sb("w13_hi", [P, 2, KE, BLOCKS * F], F32R)
        w13_lo = sb("w13_lo", [P, 2, KE, BLOCKS * F], F32R)
        w2_hi = sb("w2_hi", [P, BLOCKS, E], F32R)
        w2_lo = sb("w2_lo", [P, BLOCKS, E], F32R)
        gw = sb("gw", [P, KE, EXPERTS])
        gw_hi = sb("gw_hi", [P, KE, EXPERTS], F32R)
        gw_lo = sb("gw_lo", [P, KE, EXPERTS], F32R)
        bqk = sb("bqk", [P, 2, KE])
        vd_bias = sb("vd_bias", [P, E + DP])
        ln_g = sb("ln_g", [P, DP])
        ln_b = sb("ln_b", [P, DP])
        dp_w2 = sb("dp_w2", [P, DP])
        bo = sb("bo", [P, E])
        small = sb("small", [P, 3 * GH + 2 + EXPERTS])
        g_w1, g_b1, g_w2 = (small[:, i * GH:(i + 1) * GH] for i in range(3))
        dp_b2, g_b2 = small[:, 3 * GH:3 * GH + 1], small[:, 3 * GH + 1:3 * GH + 2]
        gate_bias = small[:, 3 * GH + 2:3 * GH + 2 + EXPERTS]
        ident = sb("ident", [P, P])
        causal = sb("causal", [P, CHUNK])
        before8 = sb("before8", [P, EXPERTS, EXPERTS])
        half = sb("half", [P, 1])
        minus_half = sb("minus_half", [P, TILES])
        xa = sb("xa", [P, TILES // CHUNKS, E])
        xn = sb("xn", [P, E])
        xt = sb("xt", [P, KE, CHUNK])
        st_a = sb("st_a", [P, TILES, 6])
        mv_a = sb("mv_a", [P, TILES, 2])
        ve_a = sb("ve_a", [P, TILES])
        rs_a = sb("rs_a", [P, TILES])
        qf = sb("qf", [P, CHUNK])
        qh = sb("qh", [P, CHUNK], F32R)
        ql = sb("ql", [P, CHUNK], F32R)
        vh = sb("vh", [P, TILES, E + DP])
        hidden = vh[:, :, E:E + DP]
        drift = sb("drift", [P, TILES])
        gt = sb("gt", [P, TILES, GH])
        gate = sb("gate", [P, TILES])
        q_st = sb("q_st", [P, 2, PAIRS, S], F32R)
        k_st = sb("k_st", [P, 2, PAIRS, S], F32R)
        mx = sb("mx", [P, 2, CHUNKS, GROUP, TILES])
        neg_max = sb("neg_max", [GROUP * TILES, P], F32R)
        probs = sb("probs", [P, 2, GROUP, CHUNK])
        vaug = sb("vaug", [P, TILES, H, 32])
        o_sb = sb("o_sb", [P, CHUNK])
        l_in = sb("l_in", [P, P])
        oc = sb("oc", [P, 2, KE, Q])
        lb = sb("lb", [P, KE, Q])
        x1 = sb("x1", [P, 2, QT, E])
        xn2 = sb("xn2", [P, E])
        x2h = sb("x2h", [P, 2, KE, Q], F32R)
        x2l = sb("x2l", [P, 2, KE, Q], F32R)
        st_c = sb("st_c", [P, QT, 6])
        mv_c = sb("mv_c", [P, QT, 2])
        ve_c = sb("ve_c", [P, QT])
        rs_c = sb("rs_c", [P, QT])
        th = sb("th", [P, QT, EXPERTS])
        sc = sb("sc", [P, QT, EXPERTS])
        grp = sb("grp", [P, QT, EXPERTS // 2])
        cmp_a = sb("cmp_a", [P, QT, EXPERTS, EXPERTS])
        cmp_b = sb("cmp_b", [P, QT, EXPERTS, EXPERTS])
        rank = sb("rank", [P, QT, EXPERTS])
        rank_g = sb("rank_g", [P, QT, EXPERTS // 2])
        sel = sb("sel", [P, QT, EXPERTS])
        den = sb("den", [P, QT])
        rden = sb("rden", [P, QT])
        ew = sb("ew", [P, QT, EXPERTS])
        ewt = sb("ewt", [EXPERTS, Q])
        ewb = sb("ewb", [P, EXPERTS, Q])
        act_t = sb("act_t", [P, 2, Q])
        h_hi = sb("h_hi", [P, 2, Q], F32R)
        h_lo = sb("h_lo", [P, 2, Q], F32R)
        yt = lb

        ps_s = psum("ps_s", [P, 2, CHUNK])
        ps_m = psum("ps_m", [P, 2, CHUNK])
        ps_o = psum("ps_o", [P, CHUNK])
        ps_a = psum("ps_a", [P, CHUNK])
        ps_c = psum("ps_c", [P, CHUNK])
        ps_y = psum("ps_y", [P, KE, Q])

        wa_in, wf_split = sem("wa_in"), sem("wf_split")
        wf_in = [sem(f"wf_in{i}") for i in range(2)]
        gw_split, const_set, ones_set = sem("gw_split"), sem("const_set"), sem("ones_set")
        x_ld, a_stat, a_var, a_rstd, a_xn = (sem(n) for n in ("x_ld", "a_stat", "a_var", "a_rstd", "a_xn"))
        a_full, a_free, q_split, qk_st = (sem(n) for n in ("a_full", "a_free", "q_split", "qk_st"))
        g_dve, g_pool, g_act = sem("g_dve"), sem("g_pool"), sem("g_act")
        va_built = sem("va_built")
        st_in = [sem(f"st_in{i}") for i in range(2)]
        m_full = [sem(f"m_full{i}") for i in range(2)]
        m_free = [sem(f"m_free{i}") for i in range(2)]
        mx_done, nm_out = sem("mx_done"), sem("nm_out")
        nm_in = [sem(f"nm_in{i}") for i in range(2)]
        s_full, s_free, p_masked, pv_done = (sem(n) for n in ("s_full", "s_free", "p_masked", "pv_done"))
        o_free, o_st = sem("o_free"), sem("o_st")
        l_ld, l_rec, l_st = sem("l_ld"), sem("l_rec"), sem("l_st")
        c_ld = [sem(f"c_ld{i}") for i in range(2)]
        c_norm, c_stat, c_var, c_rstd, c_xn, c_hi = (
            sem(n) for n in ("c_norm", "c_stat", "c_var", "c_rstd", "c_xn", "c_hi"))
        c_full, c_free, route, ew_st, ew_ld = (sem(n) for n in ("c_full", "c_free", "route", "ew_st", "ew_ld"))
        h_prod = sem("h_prod")
        h_tanh, h_up, h_ready, y_full, y_free, out_st = (
            sem(n) for n in ("h_tanh", "h_up", "h_ready", "y_full", "y_free", "out_st"))

        N_ATTN_LOADS = 14
        FFN_CHUNKS = 6
        N_CONST = 8

        def fence(eng):
            eng.nop(nofuse=True)

        def turns(eng, steps):
            def go(items, b):
                for it in items:
                    if it[0] in steps:
                        steps[it[0]](b + it[1], *it[2:])
            go(START, -1)
            go(batch_items(True, False), 0)
            go(batch_items(True, True), 1)
            with eng.Fori(2, B - 1, 1) as b:
                go(batch_items(True, True), b)
            go(batch_items(False, True), B - 1)
            go([("PV", 0, GROUPS - 1, NSTEP - 1), ("OE", 0, GROUPS - 1, CHUNKS - 1)], B - 1)
            go(END, B)

        START = ([("AX", 1, 0), ("AS", 1, 0), ("INIT", 1)]
                 + [(it[0], 1) + it[1:] for it in side_items(True, False)[2:]]
                 + [("VA", 1, g) for g in range(GROUPS - 1)]
                 + [("LD", 1, 0)] + [("M", 1, 0, u) for u in range(len(MAXU))] + [("MT", 1, 0)]
                 + [("WF", 1)])
        END = [(it[0], -1) + it[1:] for it in side_items(False, True)]

        def a_use(item, *args):
            c = args[0] // (TILES // CHUNKS) if item != "AQ" else args[0]
            base = c * (A_USES // CHUNKS)
            t = args[0] % (TILES // CHUNKS)
            n = TILES // CHUNKS
            return base + {"AT": lambda: t, "AV": lambda: n + t, "AQ": lambda: 2 * n + args[1]}[item]()

        c_order = {}
        for it in side_items(False, True):
            if it[0] in ("CW", "CT", "CG", "CE", "H", "F"):
                c_order[it[:3] if it[0] in ("CW", "CT", "H") else it[:2]] = len(c_order)
        assert len(c_order) == CD_USES
        for project in (True, False):
            again = [it[:3] if it[0] in ("CW", "CT", "H") else it[:2] for it in side_items(project, True)
                     if it[0] in ("CW", "CT", "CG", "CE", "H", "F")]
            assert again == sorted(c_order, key=c_order.get)

        def c_use(*key):
            return c_order[key]

        block = ctx.enter_context(nc.Block())

        def ffn_halves(i):
            if i < 4:
                return w13_hi[:, i // 2, i % 2, :], w13_lo[:, i // 2, i % 2, :]
            b0 = (i - 4) * BLOCKS // 2
            return tuple(w[:, b0:b0 + BLOCKS // 2, :].rearrange("p a b -> p (a b)") for w in (w2_hi, w2_lo))

        @block.sync
        def _(sp):
            def row(name, lo, hi):
                return ins[name][lo:hi].partition_broadcast(P)

            sp.dma_start(wvd[:, :, 0:E], ins["Wv"].rearrange("(k p) n -> p k n", p=P)).then_inc(wa_in, 16)
            sp.dma_start(wvd[:, :, E:], ins["dp_w1"].rearrange("(k p) n -> p k n", p=P)).then_inc(wa_in, 16)
            sp.dma_start(wq[:], ins["Wq"].rearrange("(k p) n -> p k n", p=P)).then_inc(wa_in, 16)
            sp.dma_start(wk[:], ins["Wk"].rearrange("(k p) n -> p k n", p=P)).then_inc(wa_in, 16)
            sp.dma_start(wo[:], ins["Wo"].rearrange("(k p) n -> p k n", p=P)).then_inc(wa_in, 16)
            sp.dma_start(gw[:], ins["gate_w"].rearrange("(k p) n -> p k n", p=P)).then_inc(wa_in, 16)
            sp.dma_start(bqk[:], ins["bqk"]).then_inc(wa_in, 16)
            sp.dma_start(vd_bias[:, 0:E], row("bv", 0, E)).then_inc(wa_in, 16)
            sp.dma_start(vd_bias[:, E:], row("dp_b1", 0, DP)).then_inc(wa_in, 16)
            sp.dma_start(ln_g[:], row("ln_g", 0, DP)).then_inc(wa_in, 16)
            sp.dma_start(ln_b[:], row("ln_b", 0, DP)).then_inc(wa_in, 16)
            sp.dma_start(dp_w2[:], row("dp_w2", 0, DP)).then_inc(wa_in, 16)
            sp.dma_start(bo[:], row("bo", 0, E)).then_inc(wa_in, 16)
            sp.dma_start(small[:], row("small", 0, small.shape[1])).then_inc(wa_in, 16)

            def load_x(n, c):
                if c >= CHUNKS:
                    return
                sp.wait_ge(a_xn, n * TILES + c * (TILES // CHUNKS))
                fence(sp)
                sp.dma_start(xa[:], x_in[bass.ds(n * S + c * CHUNK, CHUNK), :].rearrange(
                    "(t p) e -> p t e", p=P)).then_inc(x_ld, 16)

            def store_qk(n, c, u):
                use = n * (2 * KE * CHUNKS) + c * 2 * KE + u
                sp.wait_ge(q_split, 2 * use + 2)
                fence(sp)
                kind, m = divmod(u, KE)
                for half_, t in ((0, qh), (1, ql)):
                    r = n * (4 * E) + (2 * kind + half_) * E + m * P
                    sp.dma_start(qk_s[bass.ds(r, P), c * CHUNK:(c + 1) * CHUNK],
                                 t[:].bitcast(F32)).then_inc(qk_st, 16)

            def load_stacks(n, g):
                gi, buf = n * GROUPS + g, g % 2
                if isinstance(n, int) and n == 0:
                    sp.wait_ge(ones_set, 2)
                    fence(sp)
                sp.wait_ge(qk_st, (n + 1) * (2 * KE * CHUNKS * 2 * 16))
                fence(sp)
                sp.wait_ge(s_full, (gi - 1) * (2 * NSTEP) if not isinstance(gi, int) else max(gi - 1, 0) * 2 * NSTEP)
                fence(sp)
                for dst, kinds in ((q_st, (0, 0, 1)), (k_st, (2, 3, 2))):
                    for term, kind in enumerate(kinds):
                        rows = qk_s[bass.ds(n * (4 * E) + kind * E + g * GROUP * DH, GROUP * DH), :]
                        rows = rows.rearrange("(p j d) s -> j d p s", j=2, d=DH)
                        for j in range(2):
                            r = 64 * j + DH * term
                            sp.dma_start(dst[r:r + DH, buf, :, :].bitcast(F32), rows[j]).then_inc(st_in[buf], 16)

            def move_max(n, g):
                gi, buf = n * GROUPS + g, g % 2
                sp.wait_ge(m_free[0], (gi + 1) * (MAX_PER_BANK + 1))
                fence(sp)
                sp.dma_start(nm_s[bass.ds(gi * GROUP * TILES, GROUP * TILES), :], neg_max[:].bitcast(F32)).then_inc(
                    nm_out, 16)
                sp.wait_ge(nm_out, (gi + 1) * 16)
                fence(sp)
                rows = nm_s[bass.ds(gi * GROUP * TILES, GROUP * TILES), :].rearrange(
                    "(p j t) q -> j p (t q)", j=2, t=TILES)
                for j in range(2):
                    r = 64 * j + 3 * DH
                    sp.dma_start(q_st[r:r + 1, buf, :, :].bitcast(F32), rows[j]).then_inc(nm_in[buf], 16)

            def store_o(n, g, c):
                gi = n * GROUPS + g
                sp.wait_ge(o_free, gi * CHUNKS + c + 1)
                fence(sp)
                sp.dma_start(o_s[bass.ds(gi * P, P), c * CHUNK:(c + 1) * CHUNK], o_sb[:]).then_inc(o_st, 16)

            def load_l(n):
                sp.wait_ge(o_st, (n + 1) * (GROUPS * CHUNKS * 16))
                fence(sp)
                sp.wait_ge(l_st, n * 16)
                fence(sp)
                rows = o_s[bass.ds(n * (GROUPS * P), GROUPS * P), :].rearrange(
                    "(h r) (t q) -> h r t q", r=32, q=P)[:, DH, :, :]
                sp.dma_start(l_in[:], rows).then_inc(l_ld, 16)

            def store_l(n):
                sp.wait_ge(l_rec, n + 1)
                fence(sp)
                sp.dma_start(li_s[bass.ds(n * H, H), :].rearrange("h (t q) -> (h t) q", q=P),
                             l_in[:]).then_inc(l_st, 16)

            def load_o(n, q):
                buf = q % 2
                sp.wait_ge(l_st, (n + 1) * 16)
                fence(sp)
                sp.wait_ge(c_full, n * CD_USES + (c_use("CW", q - 2, QT - 1) + 1 if q >= 2 else 0))
                fence(sp)
                sp.wait_ge(c_norm, (n * QS + q) * 2)
                fence(sp)
                sp.wait_ge(c_full, n * CD_USES + (c_use("F", q - 2) + 1 if q >= 2 else 0))
                fence(sp)
                sp.wait_ge(out_st, (n * QS + max(q - 1, 0)) * 16)
                fence(sp)
                for m in range(KE):
                    rows = o_s[bass.ds(n * (GROUPS * P) + m * E, E), q * Q:(q + 1) * Q]
                    sp.dma_start(oc[:, buf, m, :], rows.rearrange("(h r) s -> h r s", r=32)[:, 0:DH, :]
                                 ).then_inc(c_ld[buf], 16)
                    heads = li_s[bass.ds(n * H + m * (P // DH), P // DH), q * Q:(q + 1) * Q]
                    sp.dma_start(lb[:, m, :], heads.unsqueeze(1).to_broadcast([P // DH, DH, Q])
                                 ).then_inc(c_ld[buf], 16)
                sp.dma_start(x1[:, buf, :, :], x_in[bass.ds(n * S + q * Q, Q), :].rearrange(
                    "(t p) e -> p t e", p=P)).then_inc(c_ld[buf], 16)

            def move_ew(n, q):
                sp.wait_ge(c_free, n * CD_USES + c_use("CE", q) + 1)
                fence(sp)
                sp.dma_start(ew_s[bass.ds(n * EXPERTS, EXPERTS), q * Q:(q + 1) * Q], ewt[:]).then_inc(ew_st, 16)

            def load_ew(n, q):
                sp.wait_ge(ew_st, (n * QS + q + 1) * 16)
                fence(sp)
                sp.wait_ge(h_ready, (n * QS + q) * BLOCKS)
                fence(sp)
                rows = ew_s[bass.ds(n * EXPERTS, EXPERTS), q * Q:(q + 1) * Q]
                sp.dma_start(ewb[:], rows.unsqueeze(0).to_broadcast([P, EXPERTS, Q])).then_inc(ew_ld, 16)

            def store_y(n, q):
                sp.wait_ge(c_free, n * CD_USES + c_use("F", q) + 1)
                fence(sp)
                sp.dma_start(out[bass.ds(n * S + q * Q, Q), :].rearrange("(t p) e -> p t e", p=P),
                             x1[:, q % 2, :, :]).then_inc(out_st, 16)

            def first_expert(n, q, i, e):
                if i == 0:
                    load_ew(n, q)

            def load_ffn(n):
                for i in range(FFN_CHUNKS):
                    if i >= 2:
                        sp.wait_ge(wf_split, 2 * (i - 1))
                    sp.dma_start(probs[:, i % 2, 0:3, :].rearrange("p a b -> p (a b)")[:, 0:BLOCKS * F],
                                 ins["wf"][i]).then_inc(wf_in[i % 2], 16)

            turns(sp, {"AX": load_x, "AQ": store_qk, "LD": load_stacks, "MT": move_max, "OE": store_o,
                       "CL": load_l, "CR": store_l, "CO": load_o, "CE": move_ew, "H": first_expert,
                       "F": store_y, "WF": load_ffn})
            sp.wait_ge(out_st, B * QS * 16)

        @block.gpsimd
        def _(pool):
            nc.gpsimd.memset(ident[:], 0.0).then_inc(const_set, 1)
            nc.gpsimd.memset(causal[:], 0.0).then_inc(const_set, 1)
            nc.gpsimd.memset(before8[:], 1.0).then_inc(const_set, 1)
            nc.gpsimd.memset(minus_half[:], -0.5).then_inc(const_set, 1)
            nc.gpsimd.memset(half[:], 0.5).then_inc(const_set, 1)
            pool.wait_ge(const_set, 5)
            nc.gpsimd.affine_select(out=ident[:], in_=ident[:], compare_op=ALU.not_equal, fill=1.0, base=0,
                                    pattern=[[-1, P]], channel_multiplier=1).then_inc(const_set, 1)
            diag = causal[:, CHUNK - P:]
            nc.gpsimd.affine_select(out=diag, in_=diag, compare_op=ALU.is_ge, fill=NEG, base=0,
                                    pattern=[[-1, P]], channel_multiplier=1).then_inc(const_set, 1)
            nc.gpsimd.affine_select(out=before8[:], in_=before8[:], compare_op=ALU.is_gt, fill=0.0, base=0,
                                    pattern=[[1, EXPERTS], [-1, EXPERTS]], channel_multiplier=0
                                    ).then_inc(const_set, 1)

            pool.wait_ge(const_set, N_CONST)

            def set_ones(n):
                nc.gpsimd.memset(k_st[:].bitcast(F32), 1.0).then_inc(ones_set, 1)
                nc.gpsimd.memset(vaug[:], 1.0).then_inc(ones_set, 1)

            def rstd_a(n, c):
                pool.wait_ge(a_var, n * CHUNKS + c + 1)
                ts = slice(c * TILES // CHUNKS, (c + 1) * TILES // CHUNKS)
                nc.gpsimd.tensor_tensor(rs_a[:, ts], ve_a[:, ts], minus_half[:, ts], ALU.pow).then_inc(a_rstd, 1)

            def split_qk(n, c, u):
                use = n * (2 * KE * CHUNKS) + c * 2 * KE + u
                pool.wait_ge(a_free, n * A_USES + a_use("AQ", c, u) + 1)
                pool.wait_ge(qk_st, use * 32)
                fence(pool)
                nc.gpsimd.tensor_copy(qh[:], qf[:]).then_inc(q_split, 1)
                pool.wait_ge(q_split, 2 * use + 1)
                nc.gpsimd.tensor_tensor(ql[:], qf[:], qh[:], ALU.subtract).then_inc(q_split, 1)

            G_POOL = 7

            def gate_rstd(n):
                pool.wait_ge(g_dve, n * 5 + 1)
                nc.gpsimd.tensor_tensor(rs_a[:], ve_a[:], minus_half[:], ALU.pow).then_inc(g_pool, 1)

            def gate_scale(n):
                pool.wait_ge(g_dve, n * 5 + 2)
                nc.gpsimd.tensor_tensor(hidden, hidden, ln_g[:].unsqueeze(1).to_broadcast([P, TILES, DP]),
                                        ALU.mult).then_inc(g_pool, 1)
                pool.wait_ge(g_pool, n * G_POOL + 2)
                nc.gpsimd.tensor_tensor(hidden, hidden, ln_b[:].unsqueeze(1).to_broadcast([P, TILES, DP]),
                                        ALU.add).then_inc(g_pool, 1)

            def gate_dot1(n):
                pool.wait_ge(g_act, n * 3 + 1)
                nc.gpsimd.tensor_tensor(hidden, hidden, dp_w2[:].unsqueeze(1).to_broadcast([P, TILES, DP]),
                                        ALU.mult).then_inc(g_pool, 1)

            def gate_hidden(n):
                pool.wait_ge(g_dve, n * 5 + 4)
                nc.gpsimd.tensor_tensor(gt[:], drift[:].unsqueeze(2).to_broadcast([P, TILES, GH]),
                                        g_w1.unsqueeze(1).to_broadcast([P, TILES, GH]), ALU.mult
                                        ).then_inc(g_pool, 1)
                pool.wait_ge(g_pool, n * G_POOL + 5)
                nc.gpsimd.tensor_tensor(gt[:], gt[:], g_b1.unsqueeze(1).to_broadcast([P, TILES, GH]),
                                        ALU.add).then_inc(g_pool, 1)

            def gate_dot2(n):
                pool.wait_ge(g_act, n * 3 + 2)
                nc.gpsimd.tensor_tensor(gt[:], gt[:], g_w2.unsqueeze(1).to_broadcast([P, TILES, GH]),
                                        ALU.mult).then_inc(g_pool, 1)

            def build_values(n, g):
                if isinstance(n, int) and n == 0:
                    pool.wait_ge(ones_set, 2)
                pool.wait_ge(g_act, n * 3 + 3)
                if not isinstance(n, int) or n * GROUPS + g >= GROUPS:
                    pool.wait_ge(pv_done, (n * GROUPS + g - (GROUPS - 1)) * NSTEP)
                for h in range(GROUP):
                    hh = g * GROUP + h
                    last = nc.gpsimd.tensor_tensor(
                        vaug[:, :, hh, 0:DH], vh[:, :, hh * DH:(hh + 1) * DH],
                        gate[:].unsqueeze(2).to_broadcast([P, TILES, DH]), ALU.mult)
                last.then_inc(va_built, 1)

            def mask(n, g, s):
                c, kt = STEPS[s]
                if kt * P < c * CHUNK:
                    return
                pool.wait_ge(s_free, (n * GROUPS + g) * (2 * NSTEP) + 2 * s + 2)
                fence(pool)
                p = probs[:, s % 2, :, 0:P]
                nc.gpsimd.affine_select(out=p, in_=p, compare_op=ALU.is_ge, fill=0.0, base=0,
                                        pattern=[[0, GROUP], [1, P]], channel_multiplier=-1).then_inc(p_masked, 1)

            def normalise(n, q):
                buf, k = q % 2, n * QS + q
                pool.wait_ge(c_ld[buf], (n * (QS // 2) + q // 2 + 1) * (2 * KE + 1) * 16)
                nc.gpsimd.tensor_tensor(oc[:, buf, :, :], oc[:, buf, :, :], lb[:], ALU.mult).then_inc(c_norm, 1)
                nc.gpsimd.tensor_tensor(x1[:, buf, :, :], x1[:, buf, :, :],
                                        bo[:].unsqueeze(1).to_broadcast([P, QT, E]), ALU.add).then_inc(c_norm, 1)

            def rstd_c(n, q):
                pool.wait_ge(c_var, n * QS + q + 1)
                nc.gpsimd.tensor_tensor(rs_c[:], ve_c[:], minus_half[:, 0:QT], ALU.pow).then_inc(c_rstd, 1)

            def expert_halves(n, q, i, e):
                use = (n * QS + q) * BLOCKS + i
                pool.wait_ge(c_free, n * CD_USES + c_use("H", q, i) + 1)
                pool.wait_ge(y_full, use - 1 if i else use)
                if e < EXPERTS:
                    pool.wait_ge(ew_ld, (n * QS + q + 1) * 16)
                w = ewb[:, e, :] if e < EXPERTS else half[:].to_broadcast([P, Q])
                a = act_t[:, i % 2, :]
                nc.gpsimd.tensor_tensor(h_hi[:, i % 2, :], a, w, ALU.mult).then_inc(h_up, 1)
                pool.wait_ge(h_up, 2 * use + 1)
                nc.gpsimd.tensor_tensor(a, a, w, ALU.mult).then_inc(h_up, 1)
                pool.wait_ge(h_up, 2 * use + 2)
                nc.gpsimd.tensor_tensor(h_lo[:, i % 2, :], a, h_hi[:, i % 2, :], ALU.subtract).then_inc(h_ready, 1)

            def split_ffn(n):
                pool.wait_ge(wa_in, N_ATTN_LOADS * 16)
                pool.wait_ge(gw_split, 1)
                nc.gpsimd.tensor_tensor(gw_lo[:], gw[:], gw_hi[:], ALU.subtract).then_inc(gw_split, 1)
                for i in range(FFN_CHUNKS):
                    pool.wait_ge(wf_split, 2 * i + 1)
                    raw = probs[:, i % 2, 0:3, :].rearrange("p a b -> p (a b)")[:, 0:BLOCKS * F]
                    hi, lo = ffn_halves(i)
                    nc.gpsimd.tensor_tensor(lo, raw, hi, ALU.subtract).then_inc(wf_split, 1)

            turns(pool, {"INIT": set_ones, "AS": rstd_a, "AQ": split_qk, "GB": gate_rstd,
                         "GD": gate_scale, "GF": gate_dot1,
                         "GH": gate_hidden, "GJ": gate_dot2, "VA": build_values, "MSK": mask,
                         "CO": normalise, "CS": rstd_c, "H": expert_halves, "WF": split_ffn})

        @block.scalar
        def _(act):
            def copy_xt(n, t):
                act.wait_ge(a_full, n * A_USES + a_use("AT", t) + 1)
                tt = t % (TILES // CHUNKS)
                nc.scalar.copy(xt[:, :, tt * P:(tt + 1) * P], ps_a[:, 0:KE * P].rearrange(
                    "p (k s) -> p k s", k=KE)).then_inc(a_free, 1)

            def gelu1(n):
                act.wait_ge(g_pool, n * 7 + 3)
                nc.scalar.activation(hidden, hidden, ACT.Gelu).then_inc(g_act, 1)

            def gelu2(n):
                act.wait_ge(g_pool, n * 7 + 6)
                nc.scalar.activation(gt[:], gt[:], ACT.Gelu).then_inc(g_act, 1)

            def gate_tanh(n):
                act.wait_ge(g_dve, n * 5 + 5)
                act.wait_ge(va_built, n * GROUPS)
                nc.scalar.activation(gate[:], drift[:], ACT.Tanh, bias=g_b2).then_inc(g_act, 1)

            def negate_max(n, g):
                gi = n * GROUPS + g
                act.wait_ge(m_full[0], (gi + 1) * (MAX_PER_BANK + 1))
                act.wait_ge(nm_out, gi * 16)
                nc.scalar.activation(neg_max[:], ps_m[0:GROUP * TILES, 0, 0:P], ACT.Identity, scale=-1.0
                                     ).then_inc(m_free[0], 1)

            def exponent(n, g, s, p):
                gi = n * GROUPS + g
                _, cols = step_queries(*STEPS[s])
                act.wait_ge(s_full, gi * (2 * NSTEP) + 2 * s + p + 1)
                if p == 0:
                    before = gi * NSTEP + s - 1
                    if not isinstance(before, int) or before > 0:
                        act.wait_ge(pv_done, before)
                    if isinstance(gi, int) and gi == 0 and s < 2:
                        act.wait_ge(wf_split, 2 * FFN_CHUNKS)
                nc.scalar.activation(probs[:, s % 2, 2 * p:2 * p + 2, 0:cols], ps_s[:, :, 0:cols], ACT.Exp
                                     ).then_inc(s_free, 1)

            def copy_o(n, g, c):
                gi = n * GROUPS + g
                act.wait_ge(pv_done, gi * NSTEP + sum(1 for cc, _ in STEPS if cc <= c))
                act.wait_ge(o_st, (gi * CHUNKS + c) * 16)
                nc.scalar.copy(o_sb[:], ps_o[:]).then_inc(o_free, 1)

            def copy_hi(n, q, i):
                act.wait_ge(c_full, n * CD_USES + c_use("CT", q, i) + 1)
                nc.scalar.copy(x2h[:, q % 2, :, i * P:(i + 1) * P], ps_c[:, 0:KE * P].rearrange(
                    "p (k s) -> p k s", k=KE)).then_inc(c_hi, 1)

            def route_tanh(n, q):
                act.wait_ge(c_full, n * CD_USES + c_use("CG", q) + 1)
                act.wait_ge(route, (n * QS + q) * ROUTE_OPS)
                nc.scalar.activation(th[:], ps_c[:, 0:QT * EXPERTS].rearrange("p (t e) -> p t e", t=QT),
                                     ACT.Tanh, scale=0.5).then_inc(c_free, 1)

            def copy_ew(n, q):
                act.wait_ge(c_full, n * CD_USES + c_use("CE", q) + 1)
                act.wait_ge(ew_st, (n * QS + q) * 16)
                nc.scalar.copy(ewt[:], ps_c[0:EXPERTS, 0:Q]).then_inc(c_free, 1)

            def expert_tanh(n, q, i, e):
                use = (n * QS + q) * BLOCKS + i
                act.wait_ge(c_full, n * CD_USES + c_use("H", q, i) + 1)
                act.wait_ge(h_ready, use - 1 if i else use)
                nc.scalar.activation(act_t[:, i % 2, :], ps_c[:, 0:Q], ACT.Tanh, scale=0.5).then_inc(h_tanh, 1)

            def copy_y(n, q):
                act.wait_ge(y_full, (n * QS + q + 1) * BLOCKS)
                act.wait_ge(c_norm, (n * QS + q + 1) * 2 + (1 if q + 1 < QS else 0))
                nc.scalar.copy(yt[:], ps_y[:]).then_inc(y_free, 1)

            def split_ffn(n):
                act.wait_ge(wa_in, N_ATTN_LOADS * 16)
                nc.scalar.copy(gw_hi[:], gw[:]).then_inc(gw_split, 1)
                for i in range(FFN_CHUNKS):
                    act.wait_ge(wf_in[i % 2], 16 * (i // 2 + 1))
                    raw = probs[:, i % 2, 0:3, :].rearrange("p a b -> p (a b)")[:, 0:BLOCKS * F]
                    if i:
                        act.wait_ge(wf_split, 2 * i)
                    nc.scalar.copy(ffn_halves(i)[0], raw).then_inc(wf_split, 1)

            turns(act, {"AT": copy_xt, "GE": gelu1, "GI": gelu2, "GL": gate_tanh, "MT": negate_max,
                        "QK": exponent, "OE": copy_o, "CT": copy_hi, "CG": route_tanh, "CE": copy_ew,
                        "H": expert_tanh, "YE": copy_y, "WF": split_ffn})

        @block.vector
        def _(dve):
            def stats(x_of, n_tiles, st, mv, ve, s_stat, done, s_var):
                for i in range(n_tiles):
                    last = nc.vector.bn_stats(st[:, i, :], x_of(i))
                last.then_inc(s_stat, 1)
                dve.wait_ge(s_stat, 2 * done + 1)
                fence(dve)
                for i in range(n_tiles):
                    last = nc.vector.bn_aggr(mv[:, i, :], st[:, i, :])
                last.then_inc(s_stat, 1)
                dve.wait_ge(s_stat, 2 * done + 2)
                nc.vector.tensor_scalar(ve, mv[:, :, 1], EPS, None, ALU.add).then_inc(s_var, 1)

            def stats_a(n, c):
                dve.wait_ge(x_ld, (n * CHUNKS + c + 1) * 16)
                k = TILES // CHUNKS
                ts = slice(c * k, (c + 1) * k)
                stats(lambda i: xa[:, i, :], k, st_a[:, ts], mv_a[:, ts], ve_a[:, ts], a_stat,
                      n * (CHUNKS + 1) + c, a_var)

            def norm_a(n, t):
                k = TILES // CHUNKS
                if t % k == 0:
                    dve.wait_ge(a_rstd, n * CHUNKS + t // k + 1)
                dve.wait_ge(a_full, n * A_USES + (a_use("AT", t - 1) + 1 if t % k else
                                                (a_use("AQ", t // k - 1, 2 * KE - 1) + 1 if t else 0)))
                nc.vector.tensor_scalar(xn[:], xa[:, t % k, :], mv_a[:, t, 0:1], rs_a[:, t:t + 1],
                                        ALU.subtract, ALU.mult).then_inc(a_xn, 1)

            def values(n, t):
                dve.wait_ge(a_full, n * A_USES + a_use("AV", t) + 1)
                if isinstance(n, int) and n == 0 and t == 0:
                    dve.wait_ge(wa_in, N_ATTN_LOADS * 16)
                dve.wait_ge(va_built, n * GROUPS)
                nc.vector.tensor_tensor(vh[:, t, :], ps_a[:, 0:E + DP], vd_bias[:], ALU.add).then_inc(a_free, 1)

            def queries_keys(n, c, u):
                use = n * (2 * KE * CHUNKS) + c * 2 * KE + u
                kind, m = divmod(u, KE)
                dve.wait_ge(a_full, n * A_USES + a_use("AQ", c, u) + 1)
                dve.wait_ge(q_split, 2 * use)
                nc.vector.tensor_scalar(qf[:], ps_a[:], bqk[:, kind, m:m + 1], DH ** -0.5 if kind == 0 else 1.0,
                                        ALU.add, ALU.mult).then_inc(a_free, 1)

            def gate_stats(n):
                dve.wait_ge(a_free, (n + 1) * A_USES)
                stats(lambda i: hidden[:, i, :], TILES, st_a[:], mv_a[:], ve_a[:], a_stat,
                      n * (CHUNKS + 1) + CHUNKS, g_dve)

            def gate_norm(n):
                dve.wait_ge(g_pool, n * 7 + 1)
                for t in range(TILES):
                    last = nc.vector.tensor_scalar(hidden[:, t, :], hidden[:, t, :], mv_a[:, t, 0:1],
                                                   rs_a[:, t:t + 1], ALU.subtract, ALU.mult)
                last.then_inc(g_dve, 1)

            def gate_drift(n):
                dve.wait_ge(g_pool, n * 7 + 4)
                nc.vector.tensor_reduce(drift[:], hidden, X_AXIS, ALU.add).then_inc(g_dve, 1)
                dve.wait_ge(g_dve, n * 5 + 3)
                nc.vector.tensor_scalar(drift[:], drift[:], dp_b2, None, ALU.add).then_inc(g_dve, 1)

            def gate_sum(n):
                dve.wait_ge(g_pool, n * 7 + 7)
                nc.vector.tensor_reduce(drift[:], gt[:], X_AXIS, ALU.add).then_inc(g_dve, 1)

            def maximum(n, g, u):
                p, qt, kc, j = MAXU[u]
                gi = n * GROUPS + g
                use = gi * (MAX_PER_BANK + 1) if j == 0 else gi * MAX_PER_BANK
                cols, diagonal = max_keys(qt, kc)
                s = ps_m[:, j, 0:cols]
                to = mx[:, g % 2, kc, 2 * p + j, qt:qt + 1]
                if u == 0:
                    dve.wait_ge(m_full[0], (gi - 1) * (MAX_PER_BANK + 1) if not isinstance(gi, int)
                         else max(gi - 1, 0) * (MAX_PER_BANK + 1))
                dve.wait_ge(m_full[j], use + u // 2 + 1)
                if diagonal:
                    fence(dve)
                    nc.vector.tensor_tensor_reduce(out=s, in0=s, in1=causal[:, CHUNK - cols:], scale=1.0,
                                                   scalar=-3e38, op0=ALU.add, op1=ALU.max,
                                                   accum_out=to).then_inc(m_free[j], 1)
                else:
                    nc.vector.tensor_reduce(to, s, X_AXIS, ALU.max).then_inc(m_free[j], 1)

            def join_max(n, g):
                gi = n * GROUPS + g
                dve.wait_ge(m_free[0], gi * (MAX_PER_BANK + 1) + MAX_PER_BANK)
                dve.wait_ge(m_free[1], (gi + 1) * MAX_PER_BANK)
                far = slice(CHUNK // P, TILES)
                a = mx[:, g % 2, 0, :, far]
                nc.vector.tensor_tensor(a, a, mx[:, g % 2, 1, :, far], ALU.max).then_inc(mx_done, 1)

            def invert_l(n):
                dve.wait_ge(l_ld, (n + 1) * 16)
                nc.vector.reciprocal(l_in[:], l_in[:]).then_inc(l_rec, 1)

            def residual(n, q, i):
                dve.wait_ge(c_full, n * CD_USES + c_use("CW", q, i) + 1)
                dve.wait_ge(c_norm, (n * QS + q + 1) * 2)
                xx = x1[:, q % 2, i, :]
                nc.vector.tensor_tensor(xx, ps_c[:, 0:E], xx, ALU.add).then_inc(c_free, 1)

            def stats_c(n, q):
                dve.wait_ge(c_free, n * CD_USES + c_use("CW", q, QT - 1) + 1)
                stats(lambda i: x1[:, q % 2, i, :], QT, st_c[:], mv_c[:], ve_c[:], c_stat, n * QS + q, c_var)

            def norm_c(n, q, i):
                use = (n * QS + q) * QT + i
                if i == 0:
                    dve.wait_ge(c_rstd, n * QS + q + 1)
                prev = c_use("CT", q, i - 1) + 1 if i else (c_use("CT", q - 1, QT - 1) + 1 if q else 0)
                dve.wait_ge(c_full, n * CD_USES + prev)
                nc.vector.tensor_scalar(xn2[:], x1[:, q % 2, i, :], mv_c[:, i, 0:1], rs_c[:, i:i + 1],
                                        ALU.subtract, ALU.mult).then_inc(c_xn, 1)
                dve.wait_ge(c_hi, use + 1)
                nc.vector.tensor_tensor(
                    x2l[:, q % 2, :, i * P:(i + 1) * P], ps_c[:, 0:KE * P].rearrange("p (k s) -> p k s", k=KE),
                    x2h[:, q % 2, :, i * P:(i + 1) * P], ALU.subtract).then_inc(c_free, 1)

            def routing(n, q):
                base = (n * QS + q) * ROUTE_OPS
                count = [0]

                def link(instruction):
                    count[0] += 1
                    instruction.then_inc(route, 1)
                    dve.wait_ge(route, base + count[0])

                def ranks(v, n_v, to):
                    a, b_ = cmp_a[:, :, 0:n_v, 0:n_v], cmp_b[:, :, 0:n_v, 0:n_v]
                    mine = v.unsqueeze(3).to_broadcast([P, QT, n_v, n_v])
                    other = v.unsqueeze(2).to_broadcast([P, QT, n_v, n_v])
                    tri = before8[:, 0:n_v, 0:n_v].unsqueeze(1).to_broadcast([P, QT, n_v, n_v])
                    link(nc.vector.tensor_tensor(a, other, mine, ALU.is_equal))
                    link(nc.vector.tensor_tensor(a, a, tri, ALU.mult))
                    link(nc.vector.tensor_tensor(b_, other, mine, ALU.is_gt))
                    link(nc.vector.tensor_tensor(a, a, b_, ALU.add))
                    link(nc.vector.tensor_reduce(to, a, X_AXIS, ALU.add))

                dve.wait_ge(c_free, n * CD_USES + c_use("CG", q) + 1)
                link(nc.vector.tensor_scalar(th[:], th[:], 0.5, 0.5, ALU.mult, ALU.add))
                link(nc.vector.tensor_tensor(sc[:], th[:], gate_bias.unsqueeze(1).to_broadcast([P, QT, EXPERTS]),
                                             ALU.add))
                pairs = sc[:].rearrange("p t (g o) -> p t g o", o=2)
                link(nc.vector.tensor_tensor(grp[:], pairs[:, :, :, 0], pairs[:, :, :, 1], ALU.add))
                ranks(grp[:], EXPERTS // 2, rank_g[:])
                link(nc.vector.scalar_tensor_tensor(
                    out=sel[:].rearrange("p t (g o) -> p (t g) o", o=2),
                    in0=rank_g[:].rearrange("p t g -> p (t g)").unsqueeze(2).to_broadcast(
                        [P, QT * EXPERTS // 2, 2]),
                    scalar=2.0, in1=sc[:].rearrange("p t (g o) -> p (t g) o", o=2), op0=ALU.is_lt, op1=ALU.mult))
                ranks(sel[:], EXPERTS, rank[:])
                link(nc.vector.scalar_tensor_tensor(out=sel[:], in0=rank[:], scalar=2.0, in1=th[:],
                                                    op0=ALU.is_lt, op1=ALU.mult))
                link(nc.vector.tensor_reduce(den[:], sel[:], X_AXIS, ALU.add))
                link(nc.vector.tensor_scalar(den[:], den[:], 1e-20, None, ALU.add))
                link(nc.vector.reciprocal(rden[:], den[:]))
                if q:
                    dve.wait_ge(c_full, n * CD_USES + c_use("CE", q - 1) + 1)
                nc.vector.scalar_tensor_tensor(
                    out=ew[:], in0=sel[:], scalar=ROUTE_SCALE / 2,
                    in1=rden[:].unsqueeze(2).to_broadcast([P, QT, EXPERTS]), op0=ALU.mult, op1=ALU.mult
                ).then_inc(route, 1)
                assert count[0] + 1 == ROUTE_OPS

            def expert_product(n, q, i, e):
                use = (n * QS + q) * BLOCKS + i
                a = act_t[:, i % 2, :]
                dve.wait_ge(h_tanh, use + 1)
                nc.vector.scalar_tensor_tensor(out=a, in0=a, scalar=1.0, in1=ps_c[:, 0:Q],
                                               op0=ALU.add, op1=ALU.mult).then_inc(h_prod, 1)
                dve.wait_ge(h_prod, use + 1)
                nc.vector.tensor_tensor(a, a, ps_c[:, Q:2 * Q], ALU.mult).then_inc(c_free, 1)

            def finish(n, q):
                dve.wait_ge(c_full, n * CD_USES + c_use("F", q) + 1)
                xx = x1[:, q % 2, :, :]
                nc.vector.tensor_tensor(xx, ps_c[:].rearrange("p (t e) -> p t e", t=QT), xx, ALU.add
                                        ).then_inc(c_free, 1)

            turns(dve, {"AS": stats_a, "AT": norm_a, "AV": values, "AQ": queries_keys, "GA": gate_stats,
                        "GC": gate_norm, "GG": gate_drift, "GK": gate_sum, "M": maximum, "MT": join_max,
                        "CR": invert_l, "CW": residual, "CS": stats_c, "CT": norm_c, "CR2": routing,
                        "H": expert_product, "F": finish})

        @block.tensor
        def _(pe):
            pe.wait_ge(wa_in, N_ATTN_LOADS * 16)
            pe.wait_ge(const_set, N_CONST)
            mm = nc.tensor.matmul

            def turn_x(n, t):
                pe.wait_ge(a_xn, n * TILES + t + 1)
                pe.wait_ge(a_free, n * A_USES + a_use("AT", t))
                for k in range(KE):
                    last = nc.tensor.transpose(ps_a[:, k * P:(k + 1) * P], xn[:, k * P:(k + 1) * P], ident[:])
                last.then_inc(a_full, 1)

            def values(n, t):
                pe.wait_ge(a_free, n * A_USES + a_use("AV", t))
                tt = t % (TILES // CHUNKS)
                for k in range(KE):
                    last = mm(ps_a[:, 0:E + DP], xt[:, k, tt * P:(tt + 1) * P], wvd[:, k, :],
                              start=(k == 0), stop=(k == KE - 1))
                last.then_inc(a_full, 1)

            def queries_keys(n, c, u):
                kind, m = divmod(u, KE)
                w = (wq, wk)[kind]
                pe.wait_ge(a_free, n * A_USES + a_use("AQ", c, u))
                for k in range(KE):
                    last = mm(ps_a[:], w[:, k, m * P:(m + 1) * P], xt[:, k, :], start=(k == 0), stop=(k == KE - 1))
                last.then_inc(a_full, 1)

            def maximum(n, g, u):
                p, qt, kc, j = MAXU[u]
                gi, buf = n * GROUPS + g, g % 2
                use = gi * (MAX_PER_BANK + 1) if j == 0 else gi * MAX_PER_BANK
                cols, _ = max_keys(qt, kc)
                if u == 0:
                    pe.wait_ge(st_in[buf], (n * (GROUPS // 2) + g // 2 + 1) * (12 * 16))
                pe.wait_ge(m_free[j], use + u // 2)
                r = slice(64 * j, 64 * j + 3 * DH)
                mm(ps_m[:, j, 0:cols], q_st[r, buf, p, qt * P:(qt + 1) * P],
                   k_st[r, buf, p, kc * CHUNK:kc * CHUNK + cols], start=True, stop=True).then_inc(m_full[j], 1)

            def turn_max(n, g):
                gi = n * GROUPS + g
                pe.wait_ge(mx_done, gi + 1)
                pe.wait_ge(m_free[0], gi * (MAX_PER_BANK + 1) + MAX_PER_BANK)
                nc.tensor.transpose(ps_m[0:GROUP * TILES, 0, 0:P], mx[:, g % 2, 0, :, :].rearrange(
                    "p h t -> p (h t)"), ident[:]).then_inc(m_full[0], 1)

            def scores(n, g, s, p):
                gi, buf = n * GROUPS + g, g % 2
                c, kt = STEPS[s]
                q0, cols = step_queries(c, kt)
                if s == 0 and p == 0:
                    pe.wait_ge(nm_in[buf], (n * (GROUPS // 2) + g // 2 + 1) * 32)
                pe.wait_ge(s_free, gi * (2 * NSTEP) + 2 * s + p)
                for j in range(2):
                    r = slice(64 * j, 64 * j + 3 * DH + 1)
                    last = mm(ps_s[:, j, 0:cols], k_st[r, buf, p, kt * P:(kt + 1) * P],
                              q_st[r, buf, p, q0:q0 + cols], start=True, stop=True)
                last.then_inc(s_full, 1)

            def sums(n, g, s):
                gi = n * GROUPS + g
                c, kt = STEPS[s]
                q0, cols = step_queries(c, kt)
                if s == 0:
                    pe.wait_ge(va_built, gi + 1)
                if kt == 0:
                    pe.wait_ge(o_free, gi * CHUNKS + c)
                pe.wait_ge(s_free, gi * (2 * NSTEP) + 2 * s + 2)
                if kt * P >= c * CHUNK:
                    seen = sum(1 for cc, kk in STEPS[:s + 1] if kk * P >= cc * CHUNK)
                    pe.wait_ge(p_masked, gi * TILES + seen)
                for h in range(GROUP):
                    last = mm(ps_o[32 * h:32 * h + 32, q0 - c * CHUNK:], vaug[:, kt, g * GROUP + h, :],
                              probs[:, s % 2, h, 0:cols], start=(kt == 0),
                              stop=(s + 1 == NSTEP or STEPS[s + 1][0] != c))
                last.then_inc(pv_done, 1)

            def project(n, q, i):
                buf = q % 2
                pe.wait_ge(c_norm, (n * QS + q) * 2 + 1)
                pe.wait_ge(c_free, n * CD_USES + c_use("CW", q, i))
                for k in range(KE):
                    last = mm(ps_c[:, 0:E], oc[:, buf, k, i * P:(i + 1) * P], wo[:, k, :],
                              start=(k == 0), stop=(k == KE - 1))
                last.then_inc(c_full, 1)

            def turn_x2(n, q, i):
                pe.wait_ge(c_xn, (n * QS + q) * QT + i + 1)
                pe.wait_ge(c_free, n * CD_USES + c_use("CT", q, i))
                for k in range(KE):
                    last = nc.tensor.transpose(ps_c[:, k * P:(k + 1) * P], xn2[:, k * P:(k + 1) * P], ident[:])
                last.then_inc(c_full, 1)

            def parts(w_hi, w_lo, x_hi, x_lo):
                return ((w_hi, x_hi), (w_lo, x_hi), (w_hi, x_lo))

            def logits(n, q):
                buf = q % 2
                if isinstance(n, int) and n == 0 and q == 0:
                    pe.wait_ge(gw_split, 2)
                pe.wait_ge(c_free, n * CD_USES + c_use("CG", q))
                for i in range(QT):
                    ts = slice(i * P, (i + 1) * P)
                    for k in range(KE):
                        for t, (xx, w) in enumerate(((x2h, gw_hi), (x2h, gw_lo), (x2l, gw_hi))):
                            last = mm(ps_c[:, i * EXPERTS:(i + 1) * EXPERTS], xx[:, buf, k, ts], w[:, k, :],
                                      start=(k == 0 and t == 0), stop=(k == KE - 1 and t == 2))
                last.then_inc(c_full, 1)

            def turn_ew(n, q):
                pe.wait_ge(route, (n * QS + q + 1) * ROUTE_OPS)
                pe.wait_ge(c_free, n * CD_USES + c_use("CE", q))
                for i in range(QT):
                    last = nc.tensor.transpose(ps_c[0:EXPERTS, i * P:(i + 1) * P], ew[:, i, :], ident[:])
                last.then_inc(c_full, 1)

            def expert_up(n, q, i, e):
                buf = q % 2
                if isinstance(n, int) and n == 0 and q == 0 and i == 0:
                    pe.wait_ge(wf_split, 2 * FFN_CHUNKS)
                pe.wait_ge(c_free, n * CD_USES + c_use("H", q, i))
                es = slice(e * F, (e + 1) * F)
                for w in range(2):
                    for k in range(KE):
                        for t, (a, b_) in enumerate(parts(w13_hi, w13_lo, x2h, x2l)):
                            last = mm(ps_c[:, w * Q:(w + 1) * Q], a[:, w, k, es], b_[:, buf, k, :],
                                      start=(k == 0 and t == 0), stop=(k == KE - 1 and t == 2))
                last.then_inc(c_full, 1)

            def expert_down(n, q, i, e):
                use = (n * QS + q) * BLOCKS + i
                if i == 0:
                    pe.wait_ge(y_free, n * QS + q)
                pe.wait_ge(h_ready, use + 1)
                for t, (a, b_) in enumerate(parts(w2_hi, w2_lo, h_hi, h_lo)):
                    for m in range(KE):
                        last = mm(ps_y[:, m, :], a[:, e, m * P:(m + 1) * P], b_[:, i % 2, :],
                                  start=(i == 0 and t == 0 and m == 0), stop=(i == BLOCKS - 1 and t == 2),
                                  skip_group_check=True)
                last.then_inc(y_full, 1)

            def turn_y(n, q):
                pe.wait_ge(y_free, n * QS + q + 1)
                pe.wait_ge(c_free, n * CD_USES + c_use("F", q))
                for i in range(QT):
                    for k in range(KE):
                        last = nc.tensor.transpose(ps_c[:, i * E + k * P:i * E + (k + 1) * P],
                                                   yt[:, k, i * P:(i + 1) * P], ident[:])
                last.then_inc(c_full, 1)

            turns(pe, {"AT": turn_x, "AV": values, "AQ": queries_keys, "M": maximum, "MT": turn_max,
                       "QK": scores, "PV": sums, "CW": project, "CT": turn_x2, "CG": logits, "CE": turn_ew,
                       "H": expert_up, "Y": expert_down, "F": turn_y})


def kernel(**inputs):
    import concourse.bacc as bacc
    from concourse.bass_utils import run_bass_kernel_spmd

    i = {n: np.ascontiguousarray(a) for n, a in inputs.items()}
    a, f = "L0_attn_", "L0_ffn_"
    up = [np.concatenate([i[f + r].transpose(2, 0, 1).reshape(E, EXPERTS * F), i[f + s].T], axis=1)
          for r, s in (("w1", "shared_gate_w"), ("w3", "shared_up_w"))]
    down = np.concatenate([i[f + "w2"].transpose(2, 0, 1),
                           i[f + "shared_down_w"].T.reshape(SHARED, F, E).transpose(1, 0, 2)], axis=1)
    down = down.reshape(F, 2, BLOCKS // 2 * E).transpose(1, 0, 2)
    laid = {
        "x": i[a + "x"].reshape(B * S, E),
        "Wq": i[a + "Wq"], "Wk": i[a + "Wk"], "Wv": i[a + "Wv"], "Wo": i[a + "Wo"], "dp_w1": i[a + "dp_w1"],
        "gate_w": i[f + "gate_w"].T,
        "bqk": np.stack([i[a + "bq"], i[a + "bk"]]).reshape(2, KE, P).transpose(2, 0, 1),
        "bv": i[a + "bv"], "dp_b1": i[a + "dp_b1"], "ln_g": i[a + "ln_g"], "ln_b": i[a + "ln_b"],
        "dp_w2": i[a + "dp_w2"].reshape(DP), "bo": i[a + "bo"],
        "small": np.concatenate([i[a + "g_w1"].reshape(GH), i[a + "g_b1"], i[a + "g_w2"].reshape(GH),
                                 i[a + "dp_b2"], i[a + "g_b2"], i[f + "gate_bias"]]),
        "wf": np.concatenate([up[0].reshape(KE, P, BLOCKS * F), up[1].reshape(KE, P, BLOCKS * F), down]),
    }
    nc = bacc.Bacc("TRN2", target_bir_lowering=False, num_devices=1)
    arrays, ins = {}, {}
    for name, array in laid.items():
        arrays[f"in_{name}"] = np.ascontiguousarray(array)
        ins[name] = nc.dram_tensor(f"in_{name}", array.shape, mybir.dt.from_np(array.dtype),
                                   kind="ExternalInput").ap()
    out = nc.dram_tensor("out", (B * S, E), F32, kind="ExternalOutput").ap()
    build(nc, ins, out)
    r = run_bass_kernel_spmd(nc, [arrays], core_ids=[0])
    return r.results[0]["out"].reshape(B, S, E)
```

```python
from contextlib import ExitStack

import numpy as np

import concourse.bass as bass
from concourse import mybir

F32 = mybir.dt.float32
F32R = mybir.dt.float32r
ALU = mybir.AluOpType
ACT = mybir.ActivationFunctionType
X_AXIS = mybir.AxisListType.X

P = 128
B, S, E = 8, 1024, 256
H, DH = 16, 16
KE = E // P
TILES = S // P
GROUP = 4
GROUPS = H // GROUP
PAIRS = GROUP // 2
CHUNK = 512
CHUNKS = S // CHUNK
DP = 128
GH = 16
EXPERTS, F, SHARED = 8, 128, 2
BLOCKS = EXPERTS + SHARED
Q = 256
QS = S // Q
QT = Q // P
EPS = 1e-5
NEG = -1e30
TERMS = 3 * DH
ROUTE_SCALE = 2.5

STEPS = [(c, kt) for c in range(CHUNKS) for kt in range(TILES) if kt * P < (c + 1) * CHUNK]
NSTEP = len(STEPS)
MAXU = [(p, qt, kc, j) for p in range(PAIRS) for qt in range(TILES)
        for kc in range(qt // (CHUNK // P) + 1) for j in range(2)]
MAX_PER_BANK = len(MAXU) // 2

A_USES = 2 * TILES + 2 * KE * CHUNKS
C_USES = QS * (2 * QT + 3)
FFN_CHUNKS = 6
ROUTE_OPS = 19


def step_queries(c, kt):
    q0 = max(c * CHUNK, kt * P)
    return q0, (c + 1) * CHUNK - q0


def max_keys(qt, kc):
    n = min(CHUNK, (qt + 1) * P - kc * CHUNK)
    return n, kc == qt // (CHUNK // P)


LAG = {"AX": 40, "AS": 45, "AN": 14, "AV": 14, "AQ": 22, "CO": 50, "CP": 32, "CW": 17, "CS": 52, "CN": 28, "CG": 20,
       "CRA": 60, "CE": 25, "H": 15, "HH": 10, "Y": 7, "YE": 12, "F": 15}


def spread(items, lo, hi):
    total = sum(LAG.get(it[0], 10) for it in items)
    out, done = [], 0
    for it in items:
        out.append((lo + (hi - lo) * done / total, it))
        done += LAG.get(it[0], 10)
    return out


FOLLOW = {"AN": (("AT", 0.006),), "AQ": (("AL", 0.0047),),
          "CN": (("CT", 0.004), ("CU", 0.0059)), "CRA": (("CRB", 0.007), ("CRC", 0.014)),
          "H": (("HM", 0.0065), ("HW", 0.011)), "F": (("FD", 0.003),)}


def with_followers(timed):
    out = []
    for t, it in timed:
        out.append((t, it))
        out += [(t + lag, (kind,) + it[1:]) for kind, lag in FOLLOW.get(it[0], ())]
    return out


def in_order(timed):
    return [it for _, it in sorted(timed, key=lambda x: x[0])]


def projection_items(c):
    tiles = range(c * TILES // CHUNKS, (c + 1) * TILES // CHUNKS)
    out = [("AS", c)] + [("AN", t) for t in tiles]
    out += [("AX", c + 1)] if c + 1 < CHUNKS else []
    return out + [("AV", t) for t in tiles] + [("AQ", c, u) for u in range(2 * KE)]


GATE = [(k,) for k in ("GA", "GB", "GC", "GD", "GE", "GF", "GG", "GH", "GI", "GJ", "GK", "GL")]
PROJECT = (0.0, 0.24, 0.62)
GATE_SPAN = (0.63, 0.72)
FINISH_SUMS = (0.035, 0.06)
EXPERTS_SPAN = (0.2, 0.95)
OUTPUT_SPAN, FIRST_OUTPUT_SPAN = 0.145, 0.124


def projection_times():
    out = [(0.0, ("AX", 0))]
    for c in range(CHUNKS):
        out += spread(projection_items(c), PROJECT[c], PROJECT[c + 1])
    return out + spread(GATE, *GATE_SPAN)


def output_items(q):
    return ([("CO", q), ("CP", q)] + [("CW", q, i) for i in range(QT)] + [("CS", q)] + [("CN", q, i) for i in range(QT)]
            + [("CG", q), ("CRA", q), ("CE", q)])


def finish_times():
    out = [(FINISH_SUMS[0], ("CL",)), (FINISH_SUMS[1], ("CR",))]
    order = list(range(EXPERTS, BLOCKS)) + list(range(EXPERTS))
    for q in range(QS):
        start = EXPERTS_SPAN[0] + (EXPERTS_SPAN[1] - EXPERTS_SPAN[0]) * q / QS
        step = (EXPERTS_SPAN[1] - EXPERTS_SPAN[0]) / QS / BLOCKS
        before = start - (OUTPUT_SPAN if q else FIRST_OUTPUT_SPAN)
        out += spread(output_items(q), before, start)
        for i in range(BLOCKS):
            out.append((start + i * step, ("H", q, i, order[i])))
            out.append((start + (i + 1.25) * step, ("HH", q, i)))
            out.append((start + (i + 2.4) * step, ("Y", q, i, order[i])))
        out.append((start + (BLOCKS + 1.41) * step, ("YE", q)))
        out.append((start + (BLOCKS + 1.95) * step, ("F", q)))
    return out


BANK_USE = {"AN": (0.006, 0.0), "AV": (0.0, 0.0), "AQ": (0.0, 0.0047), "CW": (0.0, 0.0),
            "CN": (0.004, 0.0019), "CG": (0.0, 0.0), "CE": (0.0, 0.0), "F": (0.0, 0.003)}


def side_times(project, finish):
    timed = [(t, (it[0], 1) + it[1:]) for t, it in (projection_times() if project else [])]
    timed += [(t, (it[0], -1) + it[1:]) for t, it in (finish_times() if finish else [])]
    out, free = [], 0.0
    for t, it in sorted(timed, key=lambda x: x[0]):
        if it[0] in BANK_USE:
            begins, read = BANK_USE[it[0]]
            t = max(t, free - begins)
            free = t + begins + read + 1e-4
        out.append((t, it))
    for side in (1, -1):
        mine = [x for x in out if x[1][1] == side and x[1][0] not in ("H", "HH", "Y", "YE", "F", "AX")]
        assert mine == sorted(mine, key=lambda x: x[0])
    return with_followers(out)


def batch_items(project, finish, first=False):
    timed = []

    def add(time, kind, n, *args):
        timed.append((time, (kind, n) + args))

    timed += side_times(project, finish)
    if first:
        for i in range(FFN_CHUNKS):
            add(0.1 + 0.1 * i, "WF", 0, i)
    work = [step_queries(*s)[1] + 100 for s in STEPS]
    for g in range(GROUPS):
        has_next = g + 1 < GROUPS or project
        nxt = (0, g + 1) if g + 1 < GROUPS else (1, 0)
        lo, span = g / GROUPS, 1 / GROUPS
        for s in range(NSTEP):
            t = lo + span * sum(work[:s]) / sum(work)
            d = span * work[s] / sum(work)
            add(t, "QK", 0, g, s, 0)
            add(t + 0.45 * d, "QK", 0, g, s, 1)
            add(t + 0.451 * d, "MSK", 0, g, s)
            if g or s:
                pg, ps = (g, s - 1) if s else (g - 1, NSTEP - 1)
                add(t + 0.62 * d, "PV", 0, pg, ps)
                if ps == NSTEP - 1 or STEPS[ps + 1][1] == 0:
                    add(t + 0.621 * d, "OE", 0, pg, STEPS[ps][0])
            elif finish:
                add(t + 0.62 * d, "PV", -1, GROUPS - 1, NSTEP - 1)
                add(t + 0.621 * d, "OE", -1, GROUPS - 1, CHUNKS - 1)
            if g == 0 and s == 0:
                add(t + 0.71 * d, "VA", 0, GROUPS - 1)
            if project and g == GROUPS - 1 and s in (1, 2, 3):
                add(t + 0.1 * d, "VA", 1, s - 1)
        if has_next:
            add(lo + 0.001, "LD", *nxt)
            for u in range(len(MAXU)):
                add(lo + span * (0.13 + 0.75 * (u // 2 * 2) / len(MAXU)), "M", *nxt, u)
            add(lo + span * 0.9, "MT", *nxt)
    items = in_order(timed)
    assert not finish or items.index(("CL", -1)) > items.index(("OE", -1, GROUPS - 1, CHUNKS - 1))
    return items


def build(nc, ins, out):
    x_in = ins["x"]
    with ExitStack() as ctx:
        def sb(name, shape, dt=F32):
            return ctx.enter_context(nc.sbuf_tensor(name, shape, dt))

        def psum(name, shape):
            return ctx.enter_context(nc.psum_tensor(name, shape, F32))

        def sem(name):
            return ctx.enter_context(nc.semaphore(name))

        def dram(name, shape, dt=F32):
            return nc.dram_tensor(name, shape, dt).ap()

        qk_s = dram("qk_s", (B * 2 * H * TERMS, S))
        nm_s = dram("nm_s", (B * GROUPS * GROUP * TILES, P))
        o_s = dram("o_s", (B * GROUPS * P, S))
        li_s = dram("li_s", (B * H, S))
        ew_s = dram("ew_s", (B * EXPERTS, S))

        wq = sb("wq", [P, KE, E])
        wk = sb("wk", [P, KE, E])
        wvd = sb("wvd", [P, KE, E + DP])
        wo = sb("wo", [P, KE, E])
        w13_hi = sb("w13_hi", [P, 2, KE, BLOCKS * F], F32R)
        w13_lo = sb("w13_lo", [P, 2, KE, BLOCKS * F], F32R)
        w2_hi = sb("w2_hi", [P, BLOCKS, E], F32R)
        w2_lo = sb("w2_lo", [P, BLOCKS, E], F32R)
        gw = sb("gw", [P, KE, EXPERTS])
        gw_hi = sb("gw_hi", [P, KE, EXPERTS], F32R)
        gw_lo = sb("gw_lo", [P, KE, EXPERTS], F32R)
        bqk = sb("bqk", [P, 2, KE])
        vd_bias = sb("vd_bias", [P, E + DP])
        ln_g = sb("ln_g", [P, DP])
        ln_b = sb("ln_b", [P, DP])
        dp_w2 = sb("dp_w2", [P, DP])
        bo = sb("bo", [P, E])
        small = sb("small", [P, 3 * GH + 2 + EXPERTS])
        g_w1, g_b1, g_w2 = (small[:, i * GH:(i + 1) * GH] for i in range(3))
        dp_b2, g_b2 = small[:, 3 * GH:3 * GH + 1], small[:, 3 * GH + 1:3 * GH + 2]
        gate_bias = small[:, 3 * GH + 2:3 * GH + 2 + EXPERTS]
        ident = sb("ident", [P, P])
        causal = sb("causal", [P, CHUNK])
        before8 = sb("before8", [P, EXPERTS, EXPERTS])
        half = sb("half", [P, 1])
        minus_half = sb("minus_half", [P, TILES])
        xa = sb("xa", [P, TILES // CHUNKS, E])
        xn = sb("xn", [P, E])
        xt = sb("xt", [P, KE, CHUNK])
        st_a = sb("st_a", [P, TILES, 6])
        mv_a = sb("mv_a", [P, TILES, 2])
        ve_a = sb("ve_a", [P, TILES])
        rs_a = sb("rs_a", [P, TILES])
        qh = sb("qh", [P, 2, CHUNK], F32R)
        ql = sb("ql", [P, CHUNK], F32R)
        vh = sb("vh", [P, TILES, E + DP])
        hidden = vh[:, :, E:E + DP]
        drift = sb("drift", [P, TILES])
        gt = sb("gt", [P, TILES, GH])
        gate = sb("gate", [P, TILES])
        q_st = sb("q_st", [P, 2, PAIRS, S], F32R)
        k_st = sb("k_st", [P, 2, PAIRS, S], F32R)
        mx = sb("mx", [P, 2, CHUNKS, GROUP, TILES])
        neg_max = sb("neg_max", [GROUP * TILES, P], F32R)
        probs = sb("probs", [P, 2, GROUP, CHUNK])
        vaug = sb("vaug", [P, TILES, H, 32])
        o_sb = sb("o_sb", [P, CHUNK])
        l_in = sb("l_in", [P, P])
        oc = sb("oc", [P, 2, KE, Q])
        lb = sb("lb", [P, KE, Q])
        x1 = sb("x1", [P, 2, QT, E])
        xn2 = sb("xn2", [P, E])
        x2h = sb("x2h", [P, 2, KE, Q], F32R)
        x2l = sb("x2l", [P, 2, KE, Q], F32R)
        st_c = sb("st_c", [P, QT, 6])
        mv_c = sb("mv_c", [P, QT, 2])
        ve_c = sb("ve_c", [P, QT])
        rs_c = sb("rs_c", [P, QT])
        th = sb("th", [P, QT, EXPERTS])
        sc = sb("sc", [P, QT, EXPERTS])
        grp = sb("grp", [P, QT, EXPERTS // 2])
        cmp_a = sb("cmp_a", [P, QT, EXPERTS, EXPERTS])
        cmp_b = sb("cmp_b", [P, QT, EXPERTS, EXPERTS])
        rank = sb("rank", [P, QT, EXPERTS])
        rank_g = sb("rank_g", [P, QT, EXPERTS // 2])
        sel = sb("sel", [P, QT, EXPERTS])
        den = sb("den", [P, QT])
        rden = sb("rden", [P, QT])
        ew = sb("ew", [P, QT, EXPERTS])
        ewt = sb("ewt", [EXPERTS, Q])
        ewb = sb("ewb", [P, EXPERTS, Q])
        act_t = sb("act_t", [P, 2, Q])
        h_hi = sb("h_hi", [P, 2, Q], F32R)
        h_lo = sb("h_lo", [P, 2, Q], F32R)
        yt = lb

        ps_s = psum("ps_s", [P, 2, CHUNK])
        ps_m = psum("ps_m", [P, 2, CHUNK])
        ps_o = psum("ps_o", [P, CHUNK])
        ps_ac = psum("ps_ac", [P, CHUNK])
        ps_h = psum("ps_h", [P, CHUNK])
        ps_y = psum("ps_y", [P, KE, Q])

        wa_in, wf_split = sem("wa_in"), sem("wf_split")
        wf_in = sem("wf_in")
        gw_split, const_set, ones_set = sem("gw_split"), sem("const_set"), sem("ones_set")
        x_ld, a_stat, a_var, a_rstd, a_xn = (sem(n) for n in ("x_ld", "a_stat", "a_var", "a_rstd", "a_xn"))
        qk_hi = sem("qk_hi")
        ac_full, ac_free = sem("ac_full"), sem("ac_free")
        ql_st, qh_st = sem("ql_st"), [sem(f"qh_st{i}") for i in range(2)]
        g_dve, g_pool, g_act = sem("g_dve"), sem("g_pool"), sem("g_act")
        va_built = sem("va_built")
        st_in = [sem(f"st_in{i}") for i in range(2)]
        m_full = [sem(f"m_full{i}") for i in range(2)]
        m_free = [sem(f"m_free{i}") for i in range(2)]
        mx_done, nm_out = sem("mx_done"), sem("nm_out")
        nm_in = [sem(f"nm_in{i}") for i in range(2)]
        s_full, s_free, p_masked, pv_done = (sem(n) for n in ("s_full", "s_free", "p_masked", "pv_done"))
        o_free, o_st = sem("o_free"), sem("o_st")
        l_ld, l_rec, l_st = sem("l_ld"), sem("l_rec"), sem("l_st")
        c_ld = [sem(f"c_ld{i}") for i in range(2)]
        c_norm, c_stat, c_var, c_rstd, c_xn, c_hi = (
            sem(n) for n in ("c_norm", "c_stat", "c_var", "c_rstd", "c_xn", "c_hi"))
        route, ew_st, ew_ld = (sem(n) for n in ("route", "ew_st", "ew_ld"))
        h_full, h_free = sem("h_full"), sem("h_free")
        h_prod = sem("h_prod")
        h_cast = sem("h_cast")
        h_tanh, h_up, h_ready, y_full, y_free, out_st = (
            sem(n) for n in ("h_tanh", "h_up", "h_ready", "y_full", "y_free", "out_st"))

        N_ATTN_LOADS = 14
        N_CONST = 8

        def fence(eng):
            eng.nop(nofuse=True)

        def turns(eng, steps):
            def go(items, b):
                for it in items:
                    if it[0] in steps:
                        steps[it[0]](b + it[1], *it[2:])
            go(START, -1)
            go(batch_items(True, False, first=True), 0)
            go(batch_items(True, True), 1)
            with eng.Fori(2, B - 1, 1) as b:
                go(batch_items(True, True), b)
            go(batch_items(False, True), B - 1)
            go([("PV", 0, GROUPS - 1, NSTEP - 1), ("OE", 0, GROUPS - 1, CHUNKS - 1)], B - 1)
            go(END, B)

        START = ([("AS", 1, 0), ("INIT", 1)] + in_order(side_times(True, False))[2:]
                 + [("VA", 1, g) for g in range(GROUPS - 1)]
                 + [("LD", 1, 0)] + [("M", 1, 0, u) for u in range(len(MAXU))] + [("MT", 1, 0)])
        END = in_order(side_times(False, True))

        bank_order = {}
        for kinds in ((True, False), (True, True), (False, True)):
            used = [it for it in in_order(side_times(*kinds)) if it[0] in ("AT", "AV", "AQ", "CW", "CT", "CG", "CE", "F")]
            assert len(used) == A_USES * kinds[0] + C_USES * kinds[1]
            bank_order[kinds] = {(it[0],) + it[2:]: k for k, it in enumerate(used)}

        def bank_use(b, item):
            if isinstance(b, int):
                kinds = (b < B - 1, b >= 1)
                return A_USES * min(b + 1, B) + C_USES * max(b - 1, 0) + bank_order[kinds][item]
            return b * (A_USES + C_USES) + (A_USES - C_USES + bank_order[True, True][item])

        def a_use(n, *item):
            return bank_use(n - 1, item)

        def c_use(n, *item):
            return bank_use(n + 1, item)

        def before_c(n, q, back, *args):
            if q < back:
                n, q = n - 1, q + QS
            return 0 if isinstance(n, int) and n < 0 else c_use(n, args[0], q - back, *args[1:]) + 1

        def hidden_bank(n, i):
            return ps_m[:, 1, :] if isinstance(n, int) and n == B - 1 and i % 2 else ps_h[:]

        block = ctx.enter_context(nc.Block())

        wf_raw = ewb[:].rearrange("p e q -> p (e q)")[:, 0:BLOCKS * F]

        def ffn_halves(i):
            if i < 4:
                return w13_hi[:, i // 2, i % 2, :], w13_lo[:, i // 2, i % 2, :]
            b0 = (i - 4) * BLOCKS // 2
            return tuple(w[:, b0:b0 + BLOCKS // 2, :].rearrange("p a b -> p (a b)") for w in (w2_hi, w2_lo))

        @block.sync
        def _(sp):
            def row(name, lo, hi):
                return ins[name][lo:hi].partition_broadcast(P)

            def load_x(n, c):
                if c >= CHUNKS:
                    return
                sp.wait_ge(a_xn, n * TILES + c * (TILES // CHUNKS))
                fence(sp)
                sp.dma_start(xa[:], x_in[bass.ds(n * S + c * CHUNK, CHUNK), :].rearrange(
                    "(t p) e -> p t e", p=P)).then_inc(x_ld, 16)

            load_x(0, 0)
            sp.dma_start(wvd[:, :, 0:E], ins["Wv"].rearrange("(k p) n -> p k n", p=P)).then_inc(wa_in, 16)
            sp.dma_start(wvd[:, :, E:], ins["dp_w1"].rearrange("(k p) n -> p k n", p=P)).then_inc(wa_in, 16)
            sp.dma_start(wq[:], ins["Wq"].rearrange("(k p) n -> p k n", p=P)).then_inc(wa_in, 16)
            sp.dma_start(wk[:], ins["Wk"].rearrange("(k p) n -> p k n", p=P)).then_inc(wa_in, 16)
            sp.dma_start(wo[:], ins["Wo"].rearrange("(k p) n -> p k n", p=P)).then_inc(wa_in, 16)
            sp.dma_start(gw[:], ins["gate_w"].rearrange("(k p) n -> p k n", p=P)).then_inc(wa_in, 16)
            sp.dma_start(bqk[:], ins["bqk"]).then_inc(wa_in, 16)
            sp.dma_start(vd_bias[:, 0:E], row("bv", 0, E)).then_inc(wa_in, 16)
            sp.dma_start(vd_bias[:, E:], row("dp_b1", 0, DP)).then_inc(wa_in, 16)
            sp.dma_start(ln_g[:], row("ln_g", 0, DP)).then_inc(wa_in, 16)
            sp.dma_start(ln_b[:], row("ln_b", 0, DP)).then_inc(wa_in, 16)
            sp.dma_start(dp_w2[:], row("dp_w2", 0, DP)).then_inc(wa_in, 16)
            sp.dma_start(bo[:], row("bo", 0, E)).then_inc(wa_in, 16)
            sp.dma_start(small[:], row("small", 0, small.shape[1])).then_inc(wa_in, 16)

            def store_qk(n, c, u):
                sp.wait_ge(ac_free, a_use(n, "AQ", c, u) + 1)
                fence(sp)
                kind, m = divmod(u, KE)
                rows = qk_s[bass.ds(((n * 2 + kind) * H + m * (P // DH)) * TERMS, P // DH * TERMS), :]
                rows = rows.rearrange("(h t d) s -> t h d s", t=3, d=DH)[:, :, :, c * CHUNK:(c + 1) * CHUNK]
                for term in ((0, 1), (0, 2))[kind]:
                    sp.dma_start(rows[term], qh[:, u % 2, :].bitcast(F32)).then_inc(qh_st[u % 2], 16)
                sp.dma_start(rows[2 - kind], ql[:].bitcast(F32)).then_inc(ql_st, 16)

            def load_stacks(n, g):
                gi, buf = n * GROUPS + g, g % 2
                if isinstance(n, int) and n == 0:
                    sp.wait_ge(ones_set, 2)
                    fence(sp)
                for i in range(2):
                    sp.wait_ge(qh_st[i], (n + 1) * (KE * CHUNKS * 32))
                    fence(sp)
                sp.wait_ge(ql_st, (n + 1) * (2 * KE * CHUNKS * 16))
                fence(sp)
                fence(sp)
                sp.wait_ge(s_full, (gi - 1) * (2 * NSTEP) if not isinstance(gi, int) else max(gi - 1, 0) * 2 * NSTEP)
                fence(sp)
                for dst, kind in ((q_st, 0), (k_st, 1)):
                    rows = qk_s[bass.ds(((n * 2 + kind) * H + g * GROUP) * TERMS, GROUP * TERMS), :]
                    rows = rows.rearrange("(p j r) s -> j r p s", j=2, r=TERMS)
                    for j in range(2):
                        sp.dma_start(dst[64 * j:64 * j + TERMS, buf, :, :].bitcast(F32), rows[j]
                                     ).then_inc(st_in[buf], 16)

            def move_max(n, g):
                gi, buf = n * GROUPS + g, g % 2
                sp.wait_ge(m_free[0], (gi + 1) * (MAX_PER_BANK + 1))
                fence(sp)
                sp.dma_start(nm_s[bass.ds(gi * GROUP * TILES, GROUP * TILES), :], neg_max[:].bitcast(F32)).then_inc(
                    nm_out, 16)
                sp.wait_ge(nm_out, (gi + 1) * 16)
                fence(sp)
                rows = nm_s[bass.ds(gi * GROUP * TILES, GROUP * TILES), :].rearrange(
                    "(p j t) q -> j p (t q)", j=2, t=TILES)
                for j in range(2):
                    r = 64 * j + 3 * DH
                    sp.dma_start(q_st[r:r + 1, buf, :, :].bitcast(F32), rows[j]).then_inc(nm_in[buf], 16)

            def store_o(n, g, c):
                gi = n * GROUPS + g
                sp.wait_ge(o_free, gi * CHUNKS + c + 1)
                fence(sp)
                sp.dma_start(o_s[bass.ds(gi * P, P), c * CHUNK:(c + 1) * CHUNK], o_sb[:]).then_inc(o_st, 16)

            def load_l(n):
                sp.wait_ge(o_st, (n + 1) * (GROUPS * CHUNKS * 16))
                fence(sp)
                sp.wait_ge(l_st, n * 16)
                fence(sp)
                rows = o_s[bass.ds(n * (GROUPS * P), GROUPS * P), :].rearrange(
                    "(h r) (t q) -> h r t q", r=32, q=P)[:, DH, :, :]
                sp.dma_start(l_in[:], rows).then_inc(l_ld, 16)

            def store_l(n):
                sp.wait_ge(l_rec, n + 1)
                fence(sp)
                sp.dma_start(li_s[bass.ds(n * H, H), :].rearrange("h (t q) -> (h t) q", q=P),
                             l_in[:]).then_inc(l_st, 16)

            def load_o(n, q):
                buf = q % 2
                sp.wait_ge(l_st, (n + 1) * 16)
                fence(sp)
                sp.wait_ge(ac_full, before_c(n, q, 2, "CW", QT - 1))
                fence(sp)
                sp.wait_ge(c_norm, (n * QS + q) * 2)
                fence(sp)
                sp.wait_ge(ac_full, before_c(n, q, 2 if q != 0 else 1, "F"))
                fence(sp)
                sp.wait_ge(out_st, (n * QS + max(q - 1, 0)) * 16)
                fence(sp)
                for m in range(KE):
                    rows = o_s[bass.ds(n * (GROUPS * P) + m * E, E), q * Q:(q + 1) * Q]
                    sp.dma_start(oc[:, buf, m, :], rows.rearrange("(h r) s -> h r s", r=32)[:, 0:DH, :]
                                 ).then_inc(c_ld[buf], 16)
                    heads = li_s[bass.ds(n * H + m * (P // DH), P // DH), q * Q:(q + 1) * Q]
                    sp.dma_start(lb[:, m, :], heads.unsqueeze(1).to_broadcast([P // DH, DH, Q])
                                 ).then_inc(c_ld[buf], 16)
                sp.dma_start(x1[:, buf, :, :], x_in[bass.ds(n * S + q * Q, Q), :].rearrange(
                    "(t p) e -> p t e", p=P)).then_inc(c_ld[buf], 16)

            def move_ew(n, q):
                sp.wait_ge(ac_free, c_use(n, "CE", q) + 1)
                fence(sp)
                sp.dma_start(ew_s[bass.ds(n * EXPERTS, EXPERTS), q * Q:(q + 1) * Q], ewt[:]).then_inc(ew_st, 16)

            def load_ew(n, q):
                sp.wait_ge(ew_st, (n * QS + q + 1) * 16)
                fence(sp)
                sp.wait_ge(h_ready, (n * QS + q) * BLOCKS)
                fence(sp)
                sp.wait_ge(wf_split, 2 * FFN_CHUNKS)
                fence(sp)
                rows = ew_s[bass.ds(n * EXPERTS, EXPERTS), q * Q:(q + 1) * Q]
                sp.dma_start(ewb[:], rows.unsqueeze(0).to_broadcast([P, EXPERTS, Q])).then_inc(ew_ld, 16)

            def store_y(n, q):
                sp.wait_ge(ac_free, c_use(n, "F", q) + 1)
                fence(sp)
                sp.dma_start(out[bass.ds(n * S + q * Q, Q), :].rearrange("(t p) e -> p t e", p=P),
                             x1[:, q % 2, :, :]).then_inc(out_st, 16)

            def first_expert(n, q, i, e):
                if i == 0:
                    load_ew(n, q)

            def load_ffn(n, i):
                sp.wait_ge(wf_split, 2 * i)
                sp.dma_start(wf_raw, ins["wf"][i]).then_inc(wf_in, 16)

            turns(sp, {"AX": load_x, "AQ": store_qk, "LD": load_stacks, "MT": move_max, "OE": store_o,
                       "CL": load_l, "CR": store_l, "CO": load_o, "CE": move_ew, "H": first_expert,
                       "F": store_y, "WF": load_ffn})
            sp.wait_ge(out_st, B * QS * 16)

        @block.gpsimd
        def _(pool):
            nc.gpsimd.memset(ident[:], 0.0).then_inc(const_set, 1)
            nc.gpsimd.memset(causal[:], 0.0).then_inc(const_set, 1)
            nc.gpsimd.memset(before8[:], 1.0).then_inc(const_set, 1)
            nc.gpsimd.memset(minus_half[:], -0.5).then_inc(const_set, 1)
            nc.gpsimd.memset(half[:], 0.5).then_inc(const_set, 1)
            pool.wait_ge(const_set, 5)
            nc.gpsimd.affine_select(out=ident[:], in_=ident[:], compare_op=ALU.not_equal, fill=1.0, base=0,
                                    pattern=[[-1, P]], channel_multiplier=1).then_inc(const_set, 1)
            diag = causal[:, CHUNK - P:]
            nc.gpsimd.affine_select(out=diag, in_=diag, compare_op=ALU.is_ge, fill=NEG, base=0,
                                    pattern=[[-1, P]], channel_multiplier=1).then_inc(const_set, 1)
            nc.gpsimd.affine_select(out=before8[:], in_=before8[:], compare_op=ALU.is_gt, fill=0.0, base=0,
                                    pattern=[[1, EXPERTS], [-1, EXPERTS]], channel_multiplier=0
                                    ).then_inc(const_set, 1)

            pool.wait_ge(const_set, N_CONST)

            def set_ones(n):
                nc.gpsimd.memset(k_st[:].bitcast(F32), 1.0).then_inc(ones_set, 1)
                nc.gpsimd.memset(vaug[:], 1.0).then_inc(ones_set, 1)

            def rstd_a(n, c):
                pool.wait_ge(a_var, n * CHUNKS + c + 1)
                ts = slice(c * TILES // CHUNKS, (c + 1) * TILES // CHUNKS)
                nc.gpsimd.tensor_tensor(rs_a[:, ts], ve_a[:, ts], minus_half[:, ts], ALU.pow).then_inc(a_rstd, 1)

            G_POOL = 7

            def gate_rstd(n):
                pool.wait_ge(g_dve, n * 5 + 1)
                nc.gpsimd.tensor_tensor(rs_a[:], ve_a[:], minus_half[:], ALU.pow).then_inc(g_pool, 1)

            def gate_scale(n):
                pool.wait_ge(g_dve, n * 5 + 2)
                nc.gpsimd.tensor_tensor(hidden, hidden, ln_g[:].unsqueeze(1).to_broadcast([P, TILES, DP]),
                                        ALU.mult).then_inc(g_pool, 1)
                pool.wait_ge(g_pool, n * G_POOL + 2)
                nc.gpsimd.tensor_tensor(hidden, hidden, ln_b[:].unsqueeze(1).to_broadcast([P, TILES, DP]),
                                        ALU.add).then_inc(g_pool, 1)

            def gate_dot1(n):
                pool.wait_ge(g_act, n * 3 + 1)
                nc.gpsimd.tensor_tensor(hidden, hidden, dp_w2[:].unsqueeze(1).to_broadcast([P, TILES, DP]),
                                        ALU.mult).then_inc(g_pool, 1)

            def gate_hidden(n):
                pool.wait_ge(g_dve, n * 5 + 4)
                nc.gpsimd.tensor_tensor(gt[:], drift[:].unsqueeze(2).to_broadcast([P, TILES, GH]),
                                        g_w1.unsqueeze(1).to_broadcast([P, TILES, GH]), ALU.mult
                                        ).then_inc(g_pool, 1)
                pool.wait_ge(g_pool, n * G_POOL + 5)
                nc.gpsimd.tensor_tensor(gt[:], gt[:], g_b1.unsqueeze(1).to_broadcast([P, TILES, GH]),
                                        ALU.add).then_inc(g_pool, 1)

            def gate_dot2(n):
                pool.wait_ge(g_act, n * 3 + 2)
                nc.gpsimd.tensor_tensor(gt[:], gt[:], g_w2.unsqueeze(1).to_broadcast([P, TILES, GH]),
                                        ALU.mult).then_inc(g_pool, 1)

            def build_values(n, g):
                if isinstance(n, int) and n == 0:
                    pool.wait_ge(ones_set, 2)
                pool.wait_ge(g_act, n * 3 + 3)
                if not isinstance(n, int) or n * GROUPS + g >= GROUPS:
                    pool.wait_ge(pv_done, (n * GROUPS + g - (GROUPS - 1)) * NSTEP)
                for h in range(GROUP):
                    hh = g * GROUP + h
                    last = nc.gpsimd.tensor_tensor(
                        vaug[:, :, hh, 0:DH], vh[:, :, hh * DH:(hh + 1) * DH],
                        gate[:].unsqueeze(2).to_broadcast([P, TILES, DH]), ALU.mult)
                last.then_inc(va_built, 1)

            def mask(n, g, s):
                c, kt = STEPS[s]
                if kt * P < c * CHUNK:
                    return
                pool.wait_ge(s_free, (n * GROUPS + g) * (2 * NSTEP) + 2 * s + 2)
                fence(pool)
                p = probs[:, s % 2, :, 0:P]
                nc.gpsimd.affine_select(out=p, in_=p, compare_op=ALU.is_ge, fill=0.0, base=0,
                                        pattern=[[0, GROUP], [1, P]], channel_multiplier=-1).then_inc(p_masked, 1)

            def normalise(n, q):
                buf, k = q % 2, n * QS + q
                pool.wait_ge(c_ld[buf], (n * (QS // 2) + q // 2 + 1) * (2 * KE + 1) * 16)
                nc.gpsimd.tensor_tensor(oc[:, buf, :, :], oc[:, buf, :, :], lb[:], ALU.mult).then_inc(c_norm, 1)
                nc.gpsimd.tensor_tensor(x1[:, buf, :, :], x1[:, buf, :, :],
                                        bo[:].unsqueeze(1).to_broadcast([P, QT, E]), ALU.add).then_inc(c_norm, 1)

            def rstd_c(n, q):
                pool.wait_ge(c_var, n * QS + q + 1)
                nc.gpsimd.tensor_tensor(rs_c[:], ve_c[:], minus_half[:, 0:QT], ALU.pow).then_inc(c_rstd, 1)

            def expert_weight(n, q, i, e):
                pool.wait_ge(h_free, (n * QS + q) * BLOCKS + i + 1)
                if e < EXPERTS:
                    pool.wait_ge(ew_ld, (n * QS + q + 1) * 16)
                w = ewb[:, e, :] if e < EXPERTS else half[:].to_broadcast([P, Q])
                a = act_t[:, i % 2, :]
                nc.gpsimd.tensor_tensor(a, a, w, ALU.mult).then_inc(h_up, 1)

            def expert_low(n, q, i):
                use = (n * QS + q) * BLOCKS + i
                pool.wait_ge(h_cast, use + 1)
                a = act_t[:, i % 2, :]
                nc.gpsimd.tensor_tensor(h_lo[:, i % 2, :], a, h_hi[:, i % 2, :], ALU.subtract).then_inc(h_ready, 1)

            def split_ffn(n, i):
                if i == 0:
                    pool.wait_ge(gw_split, 1)
                    nc.gpsimd.tensor_tensor(gw_lo[:], gw[:], gw_hi[:], ALU.subtract).then_inc(gw_split, 1)
                pool.wait_ge(wf_split, 2 * i + 1)
                hi, lo = ffn_halves(i)
                nc.gpsimd.tensor_tensor(lo, wf_raw, hi, ALU.subtract).then_inc(wf_split, 1)

            turns(pool, {"INIT": set_ones, "AS": rstd_a, "GB": gate_rstd,
                         "GD": gate_scale, "GF": gate_dot1,
                         "GH": gate_hidden, "GJ": gate_dot2, "VA": build_values, "MSK": mask,
                         "CP": normalise, "CS": rstd_c, "HW": expert_weight, "HH": expert_low, "WF": split_ffn})

        @block.scalar
        def _(act):
            def copy_xt(n, t):
                act.wait_ge(ac_full, a_use(n, "AT", t) + 1)
                tt = t % (TILES // CHUNKS)
                nc.scalar.copy(xt[:, :, tt * P:(tt + 1) * P], ps_ac[:, 0:KE * P].rearrange(
                    "p (k s) -> p k s", k=KE)).then_inc(ac_free, 1)

            def queries_keys(n, c, u):
                kind, m = divmod(u, KE)
                act.wait_ge(ac_full, a_use(n, "AQ", c, u) + 1)
                act.wait_ge(qh_st[u % 2], (n * KE * CHUNKS + c * KE + u // 2) * 32)
                nc.scalar.activation(qh[:, u % 2, :], ps_ac[:], ACT.Identity, bias=bqk[:, kind, m:m + 1]
                                     ).then_inc(qk_hi, 1)

            def gelu1(n):
                act.wait_ge(g_pool, n * 7 + 3)
                nc.scalar.activation(hidden, hidden, ACT.Gelu).then_inc(g_act, 1)

            def gelu2(n):
                act.wait_ge(g_pool, n * 7 + 6)
                nc.scalar.activation(gt[:], gt[:], ACT.Gelu).then_inc(g_act, 1)

            def gate_tanh(n):
                act.wait_ge(g_dve, n * 5 + 5)
                act.wait_ge(va_built, n * GROUPS)
                nc.scalar.activation(gate[:], drift[:], ACT.Tanh, bias=g_b2).then_inc(g_act, 1)

            def negate_max(n, g):
                gi = n * GROUPS + g
                act.wait_ge(m_full[0], (gi + 1) * (MAX_PER_BANK + 1))
                act.wait_ge(nm_out, gi * 16)
                nc.scalar.activation(neg_max[:], ps_m[0:GROUP * TILES, 0, 0:P], ACT.Identity, scale=-1.0
                                     ).then_inc(m_free[0], 1)

            def exponent(n, g, s, p):
                gi = n * GROUPS + g
                _, cols = step_queries(*STEPS[s])
                act.wait_ge(s_full, gi * (2 * NSTEP) + 2 * s + p + 1)
                if p == 0:
                    before = gi * NSTEP + s - 1
                    if not isinstance(before, int) or before > 0:
                        act.wait_ge(pv_done, before)
                nc.scalar.activation(probs[:, s % 2, 2 * p:2 * p + 2, 0:cols], ps_s[:, :, 0:cols], ACT.Exp,
                                     scale=DH ** -0.5
                                     ).then_inc(s_free, 1)

            def copy_o(n, g, c):
                gi = n * GROUPS + g
                act.wait_ge(pv_done, gi * NSTEP + sum(1 for cc, _ in STEPS if cc <= c))
                act.wait_ge(o_st, (gi * CHUNKS + c) * 16)
                nc.scalar.copy(o_sb[:], ps_o[:]).then_inc(o_free, 1)

            def copy_hi(n, q, i):
                act.wait_ge(ac_full, c_use(n, "CT", q, i) + 1)
                if not isinstance(n, int) or n * QS + q >= 2:
                    act.wait_ge(h_full, (n * QS + q - 1) * BLOCKS)
                nc.scalar.copy(x2h[:, q % 2, :, i * P:(i + 1) * P], ps_ac[:, 0:KE * P].rearrange(
                    "p (k s) -> p k s", k=KE)).then_inc(c_hi, 1)

            def route_tanh(n, q):
                act.wait_ge(ac_full, c_use(n, "CG", q) + 1)
                act.wait_ge(route, (n * QS + q) * ROUTE_OPS)
                nc.scalar.activation(th[:], ps_ac[:, 0:QT * EXPERTS].rearrange("p (t e) -> p t e", t=QT),
                                     ACT.Tanh, scale=0.5).then_inc(ac_free, 1)

            def copy_ew(n, q):
                act.wait_ge(ac_full, c_use(n, "CE", q) + 1)
                act.wait_ge(ew_st, (n * QS + q) * 16)
                nc.scalar.copy(ewt[:], ps_ac[0:EXPERTS, 0:Q]).then_inc(ac_free, 1)

            def expert_tanh(n, q, i, e):
                use = (n * QS + q) * BLOCKS + i
                act.wait_ge(h_full, use + 1)
                act.wait_ge(h_ready, use - 1 if not isinstance(use, int) or use else 0)
                nc.scalar.activation(act_t[:, i % 2, :], hidden_bank(n, i)[:, 0:Q], ACT.Tanh, scale=0.5).then_inc(h_tanh, 1)

            def expert_high(n, q, i):
                use = (n * QS + q) * BLOCKS + i
                act.wait_ge(h_up, use + 1)
                act.wait_ge(y_full, use - 1 if not isinstance(use, int) or use else 0)
                nc.scalar.copy(h_hi[:, i % 2, :], act_t[:, i % 2, :]).then_inc(h_cast, 1)

            def copy_y(n, q):
                act.wait_ge(y_full, (n * QS + q + 1) * BLOCKS)
                act.wait_ge(c_norm, (n * QS + q + 1) * 2 + (1 if q + 1 < QS else 0))
                nc.scalar.copy(yt[:], ps_y[:]).then_inc(y_free, 1)

            def split_ffn(n, i):
                if i == 0:
                    act.wait_ge(wa_in, N_ATTN_LOADS * 16)
                    nc.scalar.copy(gw_hi[:], gw[:]).then_inc(gw_split, 1)
                act.wait_ge(wf_in, 16 * (i + 1))
                nc.scalar.copy(ffn_halves(i)[0], wf_raw).then_inc(wf_split, 1)

            turns(act, {"AT": copy_xt, "AQ": queries_keys, "GE": gelu1, "GI": gelu2, "GL": gate_tanh, "MT": negate_max,
                        "QK": exponent, "OE": copy_o, "CT": copy_hi, "CG": route_tanh, "CE": copy_ew,
                        "H": expert_tanh, "HH": expert_high, "YE": copy_y, "WF": split_ffn})

        @block.vector
        def _(dve):
            def stats(x_of, n_tiles, st, mv, ve, s_stat, done, s_var):
                for i in range(n_tiles):
                    last = nc.vector.bn_stats(st[:, i, :], x_of(i))
                last.then_inc(s_stat, 1)
                dve.wait_ge(s_stat, 2 * done + 1)
                fence(dve)
                for i in range(n_tiles):
                    last = nc.vector.bn_aggr(mv[:, i, :], st[:, i, :])
                last.then_inc(s_stat, 1)
                dve.wait_ge(s_stat, 2 * done + 2)
                nc.vector.tensor_scalar(ve, mv[:, :, 1], EPS, None, ALU.add).then_inc(s_var, 1)

            def stats_a(n, c):
                dve.wait_ge(x_ld, (n * CHUNKS + c + 1) * 16)
                k = TILES // CHUNKS
                ts = slice(c * k, (c + 1) * k)
                stats(lambda i: xa[:, i, :], k, st_a[:, ts], mv_a[:, ts], ve_a[:, ts], a_stat,
                      n * (CHUNKS + 1) + c, a_var)

            def norm_a(n, t):
                k = TILES // CHUNKS
                if t % k == 0:
                    dve.wait_ge(a_rstd, n * CHUNKS + t // k + 1)
                if t:
                    dve.wait_ge(ac_full, a_use(n, "AT", t - 1) + 1)
                elif not isinstance(n, int) or n >= 1:
                    dve.wait_ge(ac_full, a_use(n - 1, "AT", TILES - 1) + 1)
                nc.vector.tensor_scalar(xn[:], xa[:, t % k, :], mv_a[:, t, 0:1], rs_a[:, t:t + 1],
                                        ALU.subtract, ALU.mult).then_inc(a_xn, 1)

            def values(n, t):
                dve.wait_ge(ac_full, a_use(n, "AV", t) + 1)
                if isinstance(n, int) and n == 0 and t == 0:
                    dve.wait_ge(wa_in, N_ATTN_LOADS * 16)
                dve.wait_ge(va_built, n * GROUPS)
                nc.vector.tensor_tensor(vh[:, t, :], ps_ac[:, 0:E + DP], vd_bias[:], ALU.add).then_inc(ac_free, 1)

            def queries_keys(n, c, u):
                use = n * (2 * KE * CHUNKS) + c * 2 * KE + u
                kind, m = divmod(u, KE)
                dve.wait_ge(qk_hi, use + 1)
                dve.wait_ge(ql_st, use * 16)
                nc.vector.scalar_tensor_tensor(out=ql[:], in0=ps_ac[:], scalar=bqk[:, kind, m:m + 1],
                                               in1=qh[:, u % 2, :], op0=ALU.add, op1=ALU.subtract
                                               ).then_inc(ac_free, 1)

            def gate_stats(n):
                dve.wait_ge(ac_free, a_use(n, "AQ", CHUNKS - 1, 2 * KE - 1) + 1)
                stats(lambda i: hidden[:, i, :], TILES, st_a[:], mv_a[:], ve_a[:], a_stat,
                      n * (CHUNKS + 1) + CHUNKS, g_dve)

            def gate_norm(n):
                dve.wait_ge(g_pool, n * 7 + 1)
                for t in range(TILES):
                    last = nc.vector.tensor_scalar(hidden[:, t, :], hidden[:, t, :], mv_a[:, t, 0:1],
                                                   rs_a[:, t:t + 1], ALU.subtract, ALU.mult)
                last.then_inc(g_dve, 1)

            def gate_drift(n):
                dve.wait_ge(g_pool, n * 7 + 4)
                nc.vector.tensor_reduce(drift[:], hidden, X_AXIS, ALU.add).then_inc(g_dve, 1)
                dve.wait_ge(g_dve, n * 5 + 3)
                nc.vector.tensor_scalar(drift[:], drift[:], dp_b2, None, ALU.add).then_inc(g_dve, 1)

            def gate_sum(n):
                dve.wait_ge(g_pool, n * 7 + 7)
                nc.vector.tensor_reduce(drift[:], gt[:], X_AXIS, ALU.add).then_inc(g_dve, 1)

            def maximum(n, g, u):
                p, qt, kc, j = MAXU[u]
                gi = n * GROUPS + g
                use = gi * (MAX_PER_BANK + 1) if j == 0 else gi * MAX_PER_BANK
                cols, diagonal = max_keys(qt, kc)
                s = ps_m[:, j, 0:cols]
                to = mx[:, g % 2, kc, 2 * p + j, qt:qt + 1]
                if u == 0:
                    dve.wait_ge(m_full[0], (gi - 1) * (MAX_PER_BANK + 1) if not isinstance(gi, int)
                         else max(gi - 1, 0) * (MAX_PER_BANK + 1))
                dve.wait_ge(m_full[j], use + u // 2 + 1)
                if diagonal:
                    fence(dve)
                    nc.vector.tensor_tensor_reduce(out=s, in0=s, in1=causal[:, CHUNK - cols:], scale=1.0,
                                                   scalar=-3e38, op0=ALU.add, op1=ALU.max,
                                                   accum_out=to).then_inc(m_free[j], 1)
                else:
                    nc.vector.tensor_reduce(to, s, X_AXIS, ALU.max).then_inc(m_free[j], 1)

            def join_max(n, g):
                gi = n * GROUPS + g
                dve.wait_ge(m_free[0], gi * (MAX_PER_BANK + 1) + MAX_PER_BANK)
                dve.wait_ge(m_free[1], (gi + 1) * MAX_PER_BANK)
                far = slice(CHUNK // P, TILES)
                a = mx[:, g % 2, 0, :, far]
                nc.vector.tensor_tensor(a, a, mx[:, g % 2, 1, :, far], ALU.max).then_inc(mx_done, 1)

            def invert_l(n):
                dve.wait_ge(l_ld, (n + 1) * 16)
                nc.vector.reciprocal(l_in[:], l_in[:]).then_inc(l_rec, 1)

            def residual(n, q, i):
                dve.wait_ge(ac_full, c_use(n, "CW", q, i) + 1)
                dve.wait_ge(c_norm, (n * QS + q + 1) * 2)
                xx = x1[:, q % 2, i, :]
                nc.vector.tensor_tensor(xx, ps_ac[:, 0:E], xx, ALU.add).then_inc(ac_free, 1)

            def stats_c(n, q):
                dve.wait_ge(ac_free, c_use(n, "CW", q, QT - 1) + 1)
                stats(lambda i: x1[:, q % 2, i, :], QT, st_c[:], mv_c[:], ve_c[:], c_stat, n * QS + q, c_var)

            def norm_c(n, q, i):
                if i == 0:
                    dve.wait_ge(c_rstd, n * QS + q + 1)
                prev = c_use(n, "CT", q, i - 1) + 1 if i else before_c(n, q, 1, "CT", QT - 1)
                dve.wait_ge(ac_full, prev)
                nc.vector.tensor_scalar(xn2[:], x1[:, q % 2, i, :], mv_c[:, i, 0:1], rs_c[:, i:i + 1],
                                        ALU.subtract, ALU.mult).then_inc(c_xn, 1)

            def low_x2(n, q, i):
                dve.wait_ge(c_hi, (n * QS + q) * QT + i + 1)
                nc.vector.tensor_tensor(
                    x2l[:, q % 2, :, i * P:(i + 1) * P], ps_ac[:, 0:KE * P].rearrange("p (k s) -> p k s", k=KE),
                    x2h[:, q % 2, :, i * P:(i + 1) * P], ALU.subtract).then_inc(ac_free, 1)

            def chain(n, q, done):
                def link(instruction):
                    nonlocal done
                    done += 1
                    instruction.then_inc(route, 1)
                    dve.wait_ge(route, (n * QS + q) * ROUTE_OPS + done)
                return link

            def ranks(link, v, n_v, to):
                a, b_ = cmp_a[:, :, 0:n_v, 0:n_v], cmp_b[:, :, 0:n_v, 0:n_v]
                mine = v.unsqueeze(3).to_broadcast([P, QT, n_v, n_v])
                other = v.unsqueeze(2).to_broadcast([P, QT, n_v, n_v])
                tri = before8[:, 0:n_v, 0:n_v].unsqueeze(1).to_broadcast([P, QT, n_v, n_v])
                link(nc.vector.tensor_tensor(a, other, mine, ALU.is_equal))
                link(nc.vector.tensor_tensor(a, a, tri, ALU.mult))
                link(nc.vector.tensor_tensor(b_, other, mine, ALU.is_gt))
                link(nc.vector.tensor_tensor(a, a, b_, ALU.add))
                link(nc.vector.tensor_reduce(to, a, X_AXIS, ALU.add))

            def group_ranks(n, q):
                link = chain(n, q, 0)
                dve.wait_ge(ac_free, c_use(n, "CG", q) + 1)
                link(nc.vector.tensor_scalar(th[:], th[:], 0.5, 0.5, ALU.mult, ALU.add))
                link(nc.vector.tensor_tensor(sc[:], th[:], gate_bias.unsqueeze(1).to_broadcast([P, QT, EXPERTS]),
                                             ALU.add))
                pairs = sc[:].rearrange("p t (g o) -> p t g o", o=2)
                link(nc.vector.tensor_tensor(grp[:], pairs[:, :, :, 0], pairs[:, :, :, 1], ALU.add))
                ranks(link, grp[:], EXPERTS // 2, rank_g[:])
                link(nc.vector.scalar_tensor_tensor(
                    out=sel[:].rearrange("p t (g o) -> p (t g) o", o=2),
                    in0=rank_g[:].rearrange("p t g -> p (t g)").unsqueeze(2).to_broadcast(
                        [P, QT * EXPERTS // 2, 2]),
                    scalar=2.0, in1=sc[:].rearrange("p t (g o) -> p (t g) o", o=2),
                    op0=ALU.is_lt, op1=ALU.mult))

            def expert_ranks(n, q):
                ranks(chain(n, q, 9), sel[:], EXPERTS, rank[:])

            def weights(n, q):
                link = chain(n, q, 14)
                link(nc.vector.scalar_tensor_tensor(out=sel[:], in0=rank[:], scalar=2.0, in1=th[:],
                                                    op0=ALU.is_lt, op1=ALU.mult))
                link(nc.vector.tensor_reduce(den[:], sel[:], X_AXIS, ALU.add))
                link(nc.vector.tensor_scalar(den[:], den[:], 1e-20, None, ALU.add))
                link(nc.vector.reciprocal(rden[:], den[:]))
                dve.wait_ge(ac_full, before_c(n, q, 1, "CE"))
                nc.vector.scalar_tensor_tensor(
                    out=ew[:], in0=sel[:], scalar=ROUTE_SCALE / 2,
                    in1=rden[:].unsqueeze(2).to_broadcast([P, QT, EXPERTS]), op0=ALU.mult, op1=ALU.mult
                ).then_inc(route, 1)

            def expert_product(n, q, i, e):
                use = (n * QS + q) * BLOCKS + i
                a = act_t[:, i % 2, :]
                dve.wait_ge(h_tanh, use + 1)
                nc.vector.scalar_tensor_tensor(out=a, in0=a, scalar=1.0, in1=hidden_bank(n, i)[:, 0:Q],
                                               op0=ALU.add, op1=ALU.mult).then_inc(h_prod, 1)
                dve.wait_ge(h_prod, use + 1)
                nc.vector.tensor_tensor(a, a, hidden_bank(n, i)[:, Q:2 * Q], ALU.mult).then_inc(h_free, 1)

            def finish(n, q):
                dve.wait_ge(ac_full, c_use(n, "F", q) + 1)
                xx = x1[:, q % 2, :, :]
                nc.vector.tensor_tensor(xx, ps_ac[:].rearrange("p (t e) -> p t e", t=QT), xx, ALU.add
                                        ).then_inc(ac_free, 1)

            turns(dve, {"AS": stats_a, "AN": norm_a, "AV": values, "AL": queries_keys, "GA": gate_stats,
                        "GC": gate_norm, "GG": gate_drift, "GK": gate_sum, "M": maximum, "MT": join_max,
                        "CR": invert_l, "CW": residual, "CS": stats_c, "CN": norm_c, "CU": low_x2,
                        "CRA": group_ranks, "CRB": expert_ranks, "CRC": weights,
                        "HM": expert_product, "FD": finish})

        @block.tensor
        def _(pe):
            pe.wait_ge(const_set, N_CONST)
            mm = nc.tensor.matmul

            def turn_x(n, t):
                pe.wait_ge(a_xn, n * TILES + t + 1)
                pe.wait_ge(ac_free, a_use(n, "AT", t))
                for k in range(KE):
                    last = nc.tensor.transpose(ps_ac[:, k * P:(k + 1) * P], xn[:, k * P:(k + 1) * P], ident[:])
                last.then_inc(ac_full, 1)

            def values(n, t):
                if isinstance(n, int) and n == 0 and t == 0:
                    pe.wait_ge(wa_in, N_ATTN_LOADS * 16)
                pe.wait_ge(ac_free, a_use(n, "AV", t))
                tt = t % (TILES // CHUNKS)
                for k in range(KE):
                    last = mm(ps_ac[:, 0:E + DP], xt[:, k, tt * P:(tt + 1) * P], wvd[:, k, :],
                              start=(k == 0), stop=(k == KE - 1))
                last.then_inc(ac_full, 1)

            def queries_keys(n, c, u):
                kind, m = divmod(u, KE)
                w = (wq, wk)[kind]
                pe.wait_ge(ac_free, a_use(n, "AQ", c, u))
                for k in range(KE):
                    last = mm(ps_ac[:], w[:, k, m * P:(m + 1) * P], xt[:, k, :], start=(k == 0), stop=(k == KE - 1))
                last.then_inc(ac_full, 1)

            def maximum(n, g, u):
                p, qt, kc, j = MAXU[u]
                gi, buf = n * GROUPS + g, g % 2
                use = gi * (MAX_PER_BANK + 1) if j == 0 else gi * MAX_PER_BANK
                cols, _ = max_keys(qt, kc)
                if u == 0:
                    pe.wait_ge(st_in[buf], (n * (GROUPS // 2) + g // 2 + 1) * (4 * 16))
                pe.wait_ge(m_free[j], use + u // 2)
                r = slice(64 * j, 64 * j + 3 * DH)
                mm(ps_m[:, j, 0:cols], q_st[r, buf, p, qt * P:(qt + 1) * P],
                   k_st[r, buf, p, kc * CHUNK:kc * CHUNK + cols], start=True, stop=True).then_inc(m_full[j], 1)

            def turn_max(n, g):
                gi = n * GROUPS + g
                pe.wait_ge(mx_done, gi + 1)
                pe.wait_ge(m_free[0], gi * (MAX_PER_BANK + 1) + MAX_PER_BANK)
                nc.tensor.transpose(ps_m[0:GROUP * TILES, 0, 0:P], mx[:, g % 2, 0, :, :].rearrange(
                    "p h t -> p (h t)"), ident[:]).then_inc(m_full[0], 1)

            def scores(n, g, s, p):
                gi, buf = n * GROUPS + g, g % 2
                c, kt = STEPS[s]
                q0, cols = step_queries(c, kt)
                if s == 0 and p == 0:
                    pe.wait_ge(nm_in[buf], (n * (GROUPS // 2) + g // 2 + 1) * 32)
                pe.wait_ge(s_free, gi * (2 * NSTEP) + 2 * s + p)
                for j in range(2):
                    r = slice(64 * j, 64 * j + 3 * DH + 1)
                    last = mm(ps_s[:, j, 0:cols], k_st[r, buf, p, kt * P:(kt + 1) * P],
                              q_st[r, buf, p, q0:q0 + cols], start=True, stop=True)
                last.then_inc(s_full, 1)

            def sums(n, g, s):
                gi = n * GROUPS + g
                c, kt = STEPS[s]
                q0, cols = step_queries(c, kt)
                if s == 0:
                    pe.wait_ge(va_built, gi + 1)
                if kt == 0:
                    pe.wait_ge(o_free, gi * CHUNKS + c)
                pe.wait_ge(s_free, gi * (2 * NSTEP) + 2 * s + 2)
                if kt * P >= c * CHUNK:
                    seen = sum(1 for cc, kk in STEPS[:s + 1] if kk * P >= cc * CHUNK)
                    pe.wait_ge(p_masked, gi * TILES + seen)
                for h in range(GROUP):
                    last = mm(ps_o[32 * h:32 * h + 32, q0 - c * CHUNK:], vaug[:, kt, g * GROUP + h, :],
                              probs[:, s % 2, h, 0:cols], start=(kt == 0),
                              stop=(s + 1 == NSTEP or STEPS[s + 1][0] != c))
                last.then_inc(pv_done, 1)

            def project(n, q, i):
                buf = q % 2
                pe.wait_ge(c_norm, (n * QS + q) * 2 + 1)
                pe.wait_ge(ac_free, c_use(n, "CW", q, i))
                for k in range(KE):
                    last = mm(ps_ac[:, 0:E], oc[:, buf, k, i * P:(i + 1) * P], wo[:, k, :],
                              start=(k == 0), stop=(k == KE - 1))
                last.then_inc(ac_full, 1)

            def turn_x2(n, q, i):
                pe.wait_ge(c_xn, (n * QS + q) * QT + i + 1)
                pe.wait_ge(ac_free, c_use(n, "CT", q, i))
                for k in range(KE):
                    last = nc.tensor.transpose(ps_ac[:, k * P:(k + 1) * P], xn2[:, k * P:(k + 1) * P], ident[:])
                last.then_inc(ac_full, 1)

            def parts(w_hi, w_lo, x_hi, x_lo):
                return ((w_hi, x_hi), (w_lo, x_hi), (w_hi, x_lo))

            def logits(n, q):
                buf = q % 2
                if isinstance(n, int) and n == 0 and q == 0:
                    pe.wait_ge(gw_split, 2)
                pe.wait_ge(ac_free, c_use(n, "CG", q))
                for i in range(QT):
                    ts = slice(i * P, (i + 1) * P)
                    for k in range(KE):
                        for t, (xx, w) in enumerate(((x2h, gw_hi), (x2h, gw_lo), (x2l, gw_hi))):
                            last = mm(ps_ac[:, i * EXPERTS:(i + 1) * EXPERTS], xx[:, buf, k, ts], w[:, k, :],
                                      start=(k == 0 and t == 0), stop=(k == KE - 1 and t == 2))
                last.then_inc(ac_full, 1)

            def turn_ew(n, q):
                pe.wait_ge(route, (n * QS + q + 1) * ROUTE_OPS)
                pe.wait_ge(ac_free, c_use(n, "CE", q))
                for i in range(QT):
                    last = nc.tensor.transpose(ps_ac[0:EXPERTS, i * P:(i + 1) * P], ew[:, i, :], ident[:])
                last.then_inc(ac_full, 1)

            def expert_up(n, q, i, e):
                buf = q % 2
                if isinstance(n, int) and n == 0 and q == 0 and i == 0:
                    pe.wait_ge(wf_split, 2 * FFN_CHUNKS)
                if i == 0:
                    pe.wait_ge(ac_free, c_use(n, "CT", q, QT - 1) + 1)
                bank, use = hidden_bank(n, i), (n * QS + q) * BLOCKS + i
                if isinstance(n, int) and n == B - 1 and (q or i):
                    pe.wait_ge(h_free, use - 1)
                    pe.wait_ge(m_free[1], B * GROUPS * MAX_PER_BANK)
                else:
                    pe.wait_ge(h_free, use)
                es = slice(e * F, (e + 1) * F)
                for w in range(2):
                    for k in range(KE):
                        for t, (a, b_) in enumerate(parts(w13_hi, w13_lo, x2h, x2l)):
                            last = mm(bank[:, w * Q:(w + 1) * Q], a[:, w, k, es], b_[:, buf, k, :],
                                      start=(k == 0 and t == 0), stop=(k == KE - 1 and t == 2))
                last.then_inc(h_full, 1)

            def expert_down(n, q, i, e):
                use = (n * QS + q) * BLOCKS + i
                if i == 0:
                    pe.wait_ge(y_free, n * QS + q)
                pe.wait_ge(h_ready, use + 1)
                for t, (a, b_) in enumerate(parts(w2_hi, w2_lo, h_hi, h_lo)):
                    for m in range(KE):
                        last = mm(ps_y[:, m, :], a[:, e, m * P:(m + 1) * P], b_[:, i % 2, :],
                                  start=(i == 0 and t == 0 and m == 0), stop=(i == BLOCKS - 1 and t == 2),
                                  skip_group_check=True)
                last.then_inc(y_full, 1)

            def turn_y(n, q):
                pe.wait_ge(y_free, n * QS + q + 1)
                pe.wait_ge(ac_free, c_use(n, "F", q))
                for i in range(QT):
                    for k in range(KE):
                        last = nc.tensor.transpose(ps_ac[:, i * E + k * P:i * E + (k + 1) * P],
                                                   yt[:, k, i * P:(i + 1) * P], ident[:])
                last.then_inc(ac_full, 1)

            turns(pe, {"AT": turn_x, "AV": values, "AQ": queries_keys, "M": maximum, "MT": turn_max,
                       "QK": scores, "PV": sums, "CW": project, "CT": turn_x2, "CG": logits, "CE": turn_ew,
                       "H": expert_up, "Y": expert_down, "F": turn_y})


def kernel(**inputs):
    import concourse.bacc as bacc
    from concourse.bass_utils import run_bass_kernel_spmd

    i = {n: np.ascontiguousarray(a) for n, a in inputs.items()}
    a, f = "L0_attn_", "L0_ffn_"
    up = [np.concatenate([i[f + r].transpose(2, 0, 1).reshape(E, EXPERTS * F), i[f + s].T], axis=1)
          for r, s in (("w1", "shared_gate_w"), ("w3", "shared_up_w"))]
    down = np.concatenate([i[f + "w2"].transpose(2, 0, 1),
                           i[f + "shared_down_w"].T.reshape(SHARED, F, E).transpose(1, 0, 2)], axis=1)
    down = down.reshape(F, 2, BLOCKS // 2 * E).transpose(1, 0, 2)
    laid = {
        "x": i[a + "x"].reshape(B * S, E),
        "Wq": i[a + "Wq"], "Wk": i[a + "Wk"], "Wv": i[a + "Wv"], "Wo": i[a + "Wo"], "dp_w1": i[a + "dp_w1"],
        "gate_w": i[f + "gate_w"].T,
        "bqk": np.stack([i[a + "bq"], i[a + "bk"]]).reshape(2, KE, P).transpose(2, 0, 1),
        "bv": i[a + "bv"], "dp_b1": i[a + "dp_b1"], "ln_g": i[a + "ln_g"], "ln_b": i[a + "ln_b"],
        "dp_w2": i[a + "dp_w2"].reshape(DP), "bo": i[a + "bo"],
        "small": np.concatenate([i[a + "g_w1"].reshape(GH), i[a + "g_b1"], i[a + "g_w2"].reshape(GH),
                                 i[a + "dp_b2"], i[a + "g_b2"], i[f + "gate_bias"]]),
        "wf": np.concatenate([up[0].reshape(KE, P, BLOCKS * F), up[1].reshape(KE, P, BLOCKS * F), down]),
    }
    nc = bacc.Bacc("TRN2", target_bir_lowering=False, num_devices=1)
    arrays, ins = {}, {}
    for name, array in laid.items():
        arrays[f"in_{name}"] = np.ascontiguousarray(array)
        ins[name] = nc.dram_tensor(f"in_{name}", array.shape, mybir.dt.from_np(array.dtype),
                                   kind="ExternalInput").ap()
    out = nc.dram_tensor("out", (B * S, E), F32, kind="ExternalOutput").ap()
    build(nc, ins, out)
    r = run_bass_kernel_spmd(nc, [arrays], core_ids=[0])
    return r.results[0]["out"].reshape(B, S, E)
```
